# Optimizing a Trainium2 kernel written in Bass

```python
import numpy as np
import jax
import jax.numpy as jnp

def _softmax(x, axis=-1):
    return jax.nn.softmax(x, axis=axis)

def _gelu(x):
    return jax.nn.gelu(x, approximate=True)

def _silu(x):
    return jax.nn.silu(x)

def _sigmoid(x):
    return jax.nn.sigmoid(x)

def _layernorm(x, axis=-1, eps=1e-05):
    m = jnp.mean(x, axis=axis, keepdims=True)
    v = jnp.var(x, axis=axis, keepdims=True)
    return (x - m) / jnp.sqrt(v + eps)

def _scatter_add(tgt, idx, src, axis=0):
    return tgt.at[idx].add(src)

def _segment_sum(src, seg, n):
    return jax.ops.segment_sum(src, seg, n)
kernel_name = 'mk_flamingo_gated_d2_seqx_r8_760441'

def setup_inputs(seed: int=0):
    np.random.seed(seed)
    _w = jnp.asarray

    def _rec_inputs():
        import jax
        import jax.numpy as jnp
        _rk = jax.random.key(seed)
        x = -7.109e-05 + 0.9999 * jax.random.normal(jax.random.fold_in(_rk, 1), (4, 256, 256), jnp.float32)
        _lenS = 256 - jax.random.randint(jax.random.fold_in(_rk, 7), (4,), 0, max(1, 256 // 4) + 1, jnp.int32)
        _lenS2 = 256 - jax.random.randint(jax.random.fold_in(_rk, 8), (4,), 0, max(1, 256 // 4) + 1, jnp.int32)
        _ctx_512P = jax.random.normal(jax.random.fold_in(_rk, 11), (4, 16, 64), jnp.float32)
        _ctx_512c = jax.random.dirichlet(jax.random.fold_in(_rk, 511), 0.3 * jnp.ones((16,), jnp.float32), (4, 256))
        _ctx_512t = jnp.einsum('bsk,bkd->bsd', _ctx_512c, _ctx_512P)
        _ctx_512t = _ctx_512t * jax.lax.rsqrt(jnp.mean(jnp.square(_ctx_512t)) + 1e-12) * 0.953939
        ctx_512 = 2.81802e-05 + 1.00001 * (_ctx_512t + 0.3 * jax.random.normal(jax.random.fold_in(_rk, 611), (4, 256, 64), jnp.float32))
        _g = jax.random.normal(jax.random.fold_in(_rk, 9001), (2, 2), jnp.float32)
        _g = jnp.sign(_g) * jnp.maximum(jnp.abs(_g), 1.0) + (_g == 0) * 1.0
        g_xattn = _g[0]
        g_ffn = _g[1]
        return (x, ctx_512, g_xattn, g_ffn)
    x, ctx_512, g_xattn, g_ffn = _rec_inputs()

    def _L0_xattn_setup():
        import jax, jax.numpy as jnp
        import numpy as np
        EPS = 1e-06
        IMAGE_DIMS = 256
        key = jax.random.key(seed)
        k1, k2, k3 = jax.random.split(key, 3)
        B, I, J, D = (16, 256, 256, 64)
        p = jax.random.normal(k1, (B, I, J), dtype=jnp.float32)
        k_v = jax.random.normal(k2, (B, J, D), dtype=jnp.float32)
        W_k = jax.random.normal(k3, (D, D), dtype=jnp.float32) * (1.0 / np.sqrt(D))
        b_k = jnp.zeros((D,), dtype=jnp.float32)
        ln_gamma = jnp.ones((J,), dtype=jnp.float32)
        ln_beta = jnp.zeros((J,), dtype=jnp.float32)
        return {'p': p, 'k_v': k_v, 'W_k': W_k, 'b_k': b_k, 'ln_gamma': ln_gamma, 'ln_beta': ln_beta}
    _L0_xattn_all = _L0_xattn_setup()
    _L0_xattn_in = {k: v for k, v in _L0_xattn_all.items() if k in ('W_k', 'b_k', 'ln_gamma', 'ln_beta')}
    del _L0_xattn_all

    def _L0_ffn_setup():
        import jax, jax.numpy as jnp
        import numpy as np
        HIDDEN = 256
        NUM_EXPERTS = 32
        TOP_K = 4
        MOE_INTER = 96
        GROUP = 2
        NUM_CHUNK = NUM_EXPERTS // GROUP
        CHUNK_INTER = 128
        SMALL_SCALE = 0.05

        def _routing(x2d, gate_w):
            logits = x2d @ gate_w.T
            rw = jax.nn.softmax(logits.astype(jnp.float32), axis=-1)
            scores = jax.nn.sigmoid(logits.astype(jnp.float32))
            _, sel = jax.lax.top_k(scores, TOP_K)
            w = jnp.take_along_axis(rw, sel, axis=-1)
            w = w / w.sum(axis=-1, keepdims=True)
            return (w.astype(x2d.dtype), sel)

        def _moe(x2d, Wg, Wu, Wd, cw):
            g = jnp.einsum('th,ehi->eti', x2d, Wg)
            u = jnp.einsum('th,ehi->eti', x2d, Wu)
            a = jax.nn.silu(g) * u * cw.T[:, :, None]
            return jnp.einsum('eti,eih->th', a, Wd)
        key = jax.random.key(seed)
        ks = jax.random.split(key, 8)
        s = 0.02
        B, S = (2, 256)
        return {'hidden_states': jax.random.normal(ks[0], (B, S, HIDDEN), jnp.float32), 'gate_w': jax.random.normal(ks[1], (NUM_EXPERTS, HIDDEN), jnp.float32) * s, 'Wg': jax.random.normal(ks[2], (NUM_EXPERTS, HIDDEN, MOE_INTER), jnp.float32) * s, 'Wu': jax.random.normal(ks[3], (NUM_EXPERTS, HIDDEN, MOE_INTER), jnp.float32) * s, 'Wd': jax.random.normal(ks[4], (NUM_EXPERTS, MOE_INTER, HIDDEN), jnp.float32) * s, 'cWg': jax.random.normal(ks[5], (NUM_CHUNK, HIDDEN, CHUNK_INTER), jnp.float32) * s, 'cWu': jax.random.normal(ks[6], (NUM_CHUNK, HIDDEN, CHUNK_INTER), jnp.float32) * s, 'cWd': jax.random.normal(ks[7], (NUM_CHUNK, CHUNK_INTER, HIDDEN), jnp.float32) * s}
    _L0_ffn_all = _L0_ffn_setup()
    _L0_ffn_in = {k: v for k, v in _L0_ffn_all.items() if k in ('gate_w', 'Wg', 'Wu', 'Wd', 'cWg', 'cWu', 'cWd')}
    del _L0_ffn_all

    def _L1_xattn_setup():
        import jax, jax.numpy as jnp
        import numpy as np
        import math
        NUM_Q_HEADS = 32
        NUM_KV_HEADS = 8
        key = jax.random.key(seed)
        k1, k2, k3 = jax.random.split(key, 3)
        B, S, E = (2, 256, 256)
        kv_E = NUM_KV_HEADS * (E // NUM_Q_HEADS)
        q = jax.random.normal(k1, (B, S, E), dtype=jnp.float32)
        k = jax.random.normal(k2, (B, S, kv_E), dtype=jnp.float32)
        v = jax.random.normal(k3, (B, S, kv_E), dtype=jnp.float32)
        return {'q': q, 'k': k, 'v': v}
    _L1_xattn_all = _L1_xattn_setup()
    _L1_xattn_in = {k: v for k, v in _L1_xattn_all.items() if k in ()}
    del _L1_xattn_all

    def _L1_ffn_setup():
        import jax, jax.numpy as jnp
        import numpy as np
        D = 256
        M = 128
        E = 32
        K = 6
        G = 8
        KG = 4
        SH = 256
        SCALE = 2.5

        def _route(xf, Wr, br):
            T = xf.shape[0]
            s = jax.nn.sigmoid(xf @ Wr.T + br)
            sg = s.reshape(T, G, E // G)
            group_w = jax.lax.top_k(sg, 2)[0].sum(-1)
            top_g = jax.lax.top_k(group_w, KG)[1]
            gmask = jnp.zeros((T, G), bool).at[jnp.arange(T)[:, None], top_g].set(True)
            masked = jnp.where(gmask[:, :, None], sg, 0.0).reshape(T, E)
            idx = jax.lax.top_k(masked, K)[1]
            w = jnp.take_along_axis(s, idx, axis=1)
            w = w / (w.sum(-1, keepdims=True) + 1e-20)
            return (idx, w * SCALE)
        key = jax.random.key(seed)
        ks = jax.random.split(key, 7)
        w = 0.02
        return {'hidden_tensor': jax.random.normal(ks[0], (2, 256, D), dtype=jnp.float32), 'Wr': jax.random.normal(ks[1], (E, D), dtype=jnp.float32) * w, 'br': jax.random.normal(ks[2], (E,), dtype=jnp.float32) * w, 'W1': jax.random.normal(ks[3], (E, M, D), dtype=jnp.float32) * w, 'W2': jax.random.normal(ks[4], (E, D, M), dtype=jnp.float32) * w, 'Ws1': jax.random.normal(ks[5], (SH, D), dtype=jnp.float32) * w, 'Ws2': jax.random.normal(ks[6], (D, SH), dtype=jnp.float32) * w}
    _L1_ffn_all = _L1_ffn_setup()
    _L1_ffn_in = {k: v for k, v in _L1_ffn_all.items() if k in ('Wr', 'br', 'W1', 'W2', 'Ws1', 'Ws2')}
    del _L1_ffn_all
    return {'x': x, 'ctx_512': ctx_512, 'g_xattn': g_xattn, 'g_ffn': g_ffn, 'L0_xattn_W_k': _L0_xattn_in['W_k'], 'L0_xattn_b_k': _L0_xattn_in['b_k'], 'L0_xattn_ln_gamma': _L0_xattn_in['ln_gamma'], 'L0_xattn_ln_beta': _L0_xattn_in['ln_beta'], 'L0_ffn_gate_w': _L0_ffn_in['gate_w'], 'L0_ffn_Wg': _L0_ffn_in['Wg'], 'L0_ffn_Wu': _L0_ffn_in['Wu'], 'L0_ffn_Wd': _L0_ffn_in['Wd'], 'L0_ffn_cWg': _L0_ffn_in['cWg'], 'L0_ffn_cWu': _L0_ffn_in['cWu'], 'L0_ffn_cWd': _L0_ffn_in['cWd'], 'L1_ffn_Wr': _L1_ffn_in['Wr'], 'L1_ffn_br': _L1_ffn_in['br'], 'L1_ffn_W1': _L1_ffn_in['W1'], 'L1_ffn_W2': _L1_ffn_in['W2'], 'L1_ffn_Ws1': _L1_ffn_in['Ws1'], 'L1_ffn_Ws2': _L1_ffn_in['Ws2']}

def reference(x, ctx_512, g_xattn, g_ffn, L0_xattn_W_k, L0_xattn_b_k, L0_xattn_ln_gamma, L0_xattn_ln_beta, L0_ffn_gate_w, L0_ffn_Wg, L0_ffn_Wu, L0_ffn_Wd, L0_ffn_cWg, L0_ffn_cWu, L0_ffn_cWd, L1_ffn_Wr, L1_ffn_br, L1_ffn_W1, L1_ffn_W2, L1_ffn_Ws1, L1_ffn_Ws2):
    import jax
    import jax.numpy as jnp

    def _L0_xattn_ref(p, k_v, W_k, b_k, ln_gamma, ln_beta):
        import jax, jax.numpy as jnp
        import numpy as np
        EPS = 1e-06
        IMAGE_DIMS = 256
        kv = k_v @ W_k.T + b_k
        out = jnp.einsum('bij,bjd->bid', p, kv)
        scale = IMAGE_DIMS ** (-0.5)
        sim = jnp.einsum('bid,bjd->bij', out, kv) * scale
        mu = jnp.mean(sim, axis=-1, keepdims=True)
        var = jnp.var(sim, axis=-1, keepdims=True)
        sim = (sim - mu) * jax.lax.rsqrt(var + EPS) * ln_gamma + ln_beta
        attn = jax.nn.softmax(sim, axis=-1)
        return attn

    def _L0_ffn_ref(hidden_states, gate_w, Wg, Wu, Wd, cWg, cWu, cWd):
        import jax, jax.numpy as jnp
        import numpy as np
        HIDDEN = 256
        NUM_EXPERTS = 32
        TOP_K = 4
        MOE_INTER = 96
        GROUP = 2
        NUM_CHUNK = NUM_EXPERTS // GROUP
        CHUNK_INTER = 128
        SMALL_SCALE = 0.05

        def _routing(x2d, gate_w):
            logits = x2d @ gate_w.T
            rw = jax.nn.softmax(logits.astype(jnp.float32), axis=-1)
            scores = jax.nn.sigmoid(logits.astype(jnp.float32))
            _, sel = jax.lax.top_k(scores, TOP_K)
            w = jnp.take_along_axis(rw, sel, axis=-1)
            w = w / w.sum(axis=-1, keepdims=True)
            return (w.astype(x2d.dtype), sel)

        def _moe(x2d, Wg, Wu, Wd, cw):
            g = jnp.einsum('th,ehi->eti', x2d, Wg)
            u = jnp.einsum('th,ehi->eti', x2d, Wu)
            a = jax.nn.silu(g) * u * cw.T[:, :, None]
            return jnp.einsum('eti,eih->th', a, Wd)
        B, S, H = hidden_states.shape
        T = B * S
        x = hidden_states.reshape(T, H)
        w, sel = _routing(x, gate_w)
        rows = jnp.arange(T)[:, None]
        cw_large = jnp.zeros((T, NUM_EXPERTS), x.dtype).at[rows, sel].add(w)
        cw_small = jnp.zeros((T, NUM_CHUNK), x.dtype).at[rows, sel // GROUP].add(w)
        large = _moe(x, Wg, Wu, Wd, cw_large)
        small = _moe(x, cWg, cWu, cWd, cw_small)
        return (large + SMALL_SCALE * small).reshape(B, S, H)

    def _L1_xattn_ref(q, k, v):
        import jax, jax.numpy as jnp
        import numpy as np
        import math
        NUM_Q_HEADS = 32
        NUM_KV_HEADS = 8
        B, S, E = q.shape
        H, KV = (NUM_Q_HEADS, NUM_KV_HEADS)
        D = E // H
        G = H // KV
        scale = math.sqrt(D)
        qh = q.reshape(B, S, KV, G, D).transpose(0, 2, 3, 1, 4)
        kh = k.reshape(B, S, KV, D).transpose(0, 2, 1, 3)
        vh = v.reshape(B, S, KV, D).transpose(0, 2, 1, 3)
        scores = jnp.einsum('bkgsd,bktd->bkgst', qh, kh) / scale
        weights = jax.nn.softmax(scores, axis=-1)
        out = jnp.einsum('bkgst,bktd->bkgsd', weights, vh)
        return out.transpose(0, 3, 1, 2, 4).reshape(B, S, E)

    def _L1_ffn_ref(hidden_tensor, Wr, br, W1, W2, Ws1, Ws2):
        import jax, jax.numpy as jnp
        import numpy as np
        D = 256
        M = 128
        E = 32
        K = 6
        G = 8
        KG = 4
        SH = 256
        SCALE = 2.5

        def _route(xf, Wr, br):
            T = xf.shape[0]
            s = jax.nn.sigmoid(xf @ Wr.T + br)
            sg = s.reshape(T, G, E // G)
            group_w = jax.lax.top_k(sg, 2)[0].sum(-1)
            top_g = jax.lax.top_k(group_w, KG)[1]
            gmask = jnp.zeros((T, G), bool).at[jnp.arange(T)[:, None], top_g].set(True)
            masked = jnp.where(gmask[:, :, None], sg, 0.0).reshape(T, E)
            idx = jax.lax.top_k(masked, K)[1]
            w = jnp.take_along_axis(s, idx, axis=1)
            w = w / (w.sum(-1, keepdims=True) + 1e-20)
            return (idx, w * SCALE)
        B, Tlen, C = hidden_tensor.shape
        xf = hidden_tensor.reshape(-1, C).astype(jnp.float32)
        T = xf.shape[0]
        idx, w = _route(xf, Wr, br)
        gate = jnp.zeros((T, E), w.dtype).at[jnp.arange(T)[:, None], idx].add(w)

        def step(acc, ew):
            w1, w2, g = ew
            h = jnp.square(jax.nn.relu(xf @ w1.T)) @ w2.T
            return (acc + g[:, None] * h, None)
        acc, _ = jax.lax.scan(step, jnp.zeros_like(xf), (W1, W2, gate.T))
        moe_out = acc.reshape(B, Tlen, C).astype(hidden_tensor.dtype)
        shared = jnp.square(jax.nn.relu(hidden_tensor @ Ws1.T)) @ Ws2.T
        return shared + moe_out
    x = x + jnp.tanh(g_xattn[0]) * _L0_xattn_ref(_layernorm(x, axis=-1), ctx_512, L0_xattn_W_k, L0_xattn_b_k, L0_xattn_ln_gamma, L0_xattn_ln_beta)
    x = x + jnp.tanh(g_ffn[0]) * _L0_ffn_ref(_layernorm(x, axis=-1), L0_ffn_gate_w, L0_ffn_Wg, L0_ffn_Wu, L0_ffn_Wd, L0_ffn_cWg, L0_ffn_cWu, L0_ffn_cWd)
    x = x + jnp.tanh(g_xattn[1]) * _L1_xattn_ref(_layernorm(x, axis=-1), ctx_512, ctx_512)
    x = x + jnp.tanh(g_ffn[1]) * _L1_ffn_ref(_layernorm(x, axis=-1), L1_ffn_Wr, L1_ffn_br, L1_ffn_W1, L1_ffn_W2, L1_ffn_Ws1, L1_ffn_Ws2)
    return x

_drawn_inputs = setup_inputs


def setup_inputs(seed=0):
    import zlib

    import numpy as np

    out = dict(_drawn_inputs(seed))
    spreads = {'g_ffn': (-1.0, 0.6),
     'L0_xattn_b_k': (0.0, 2.0),
     'L0_xattn_ln_gamma': (1.0, 0.6),
     'L0_xattn_ln_beta': (0.0, 2.0)}
    factors = {'L0_xattn_W_k': 8.0,
     'L0_ffn_gate_w': 8.0,
     'L0_ffn_Wg': 8.0,
     'L0_ffn_Wu': 8.0,
     'L0_ffn_Wd': 8.0,
     'L0_ffn_cWg': 8.0,
     'L0_ffn_cWu': 8.0,
     'L0_ffn_cWd': 8.0,
     'L1_ffn_br': 64.0,
     'L1_ffn_Wr': 8.0,
     'L1_ffn_W1': 8.0,
     'L1_ffn_W2': 7.331,
     'L1_ffn_Ws1': 5.809,
     'L1_ffn_Ws2': 5.268}
    for name, (base, spread) in spreads.items():
        noise = np.random.default_rng([zlib.crc32(name.encode()), seed]).standard_normal(out[name].shape)
        drawn = base * np.exp(spread * noise) if base else spread * noise
        out[name] = jnp.asarray(drawn.astype(out[name].dtype))
    for name, factor in factors.items():
        out[name] = (out[name] * factor).astype(out[name].dtype)
    return out
```

```python
from contextlib import ExitStack

import numpy as np

import concourse.bass as bass
from concourse import mybir

ALU = mybir.AluOpType
ACT = mybir.ActivationFunctionType
AX = mybir.AxisListType
F32 = mybir.dt.float32
F32R = mybir.dt.float32r

P = 128
NB = 4
S = 256
T = NB * S
NT = T // P
HALF = 512
D = 256
KC = D // P
CD = 64
HD = 8
KV = CD // HD
G = D // HD // KV
NH = KV * G
E = 32
TOP0, TOP1, GROUPS, GTOP = 4, 6, 8, 4
INTER0, CHUNKS0 = 96, 16
SMALL_SCALE = 0.05
ROUTE_SCALE = 2.5
NC0 = E * INTER0 // P + CHUNKS0
NC1 = E + D // P
W0 = 3 * D + P
W1 = 2 * D + P
GW = 64
SENT = 3.0e38
TAKEN = -3.0e38
LN_EPS = 1e-5
SIM_EPS = 1e-6
SIM_SCALE = 1.0 / 16.0
QW = 9
QH = 8
WIN = QW * (QH - 1)
SCORE_SCALE = HD ** -0.5


def build(nc, x_d, ctx_d, ctxT_d, wkT_d, rows_d, router_d, ident_d, w0_d, w1_d, out_d):
    with ExitStack() as ctx:
        def sb(name, shape, dt=F32):
            return ctx.enter_context(nc.sbuf_tensor(name, shape, dt))

        def sem(name):
            return ctx.enter_context(nc.semaphore(name))

        psum = ctx.enter_context(nc.psum_tensor("psum", [P, 8, 512], F32))
        bank = [psum[:, i, :] for i in range(8)]

        with ExitStack() as scope:
            def early(name, shape, dt=F32):
                return scope.enter_context(nc.sbuf_tensor(name, shape, dt))

            ctxT = early("ctxT", [CD + 1, T])
            kv = early("kv", [P, NT, CD])
            kvT = early("kvT", [CD, T])
            xnT = early("xnT", [P, NB, KC, S])
            outT = early("outT", [CD, NB, S])
            ctx_hi = early("ctx_hi", [P, NT, KV, HD], F32R)
            ctx_lo = early("ctx_lo", [P, NT, KV, HD], F32R)
        qS = sb("qS", [P, KV, T], F32R)
        with ExitStack() as scope:
            q_tok = scope.enter_context(nc.sbuf_tensor("q_tok", [P, 2, KV, G, 32], F32))
            ex = scope.enter_context(nc.sbuf_tensor("ex", [P, 2, 2, 2, S], F32))
        xT_hi = sb("xT_hi", [P, KC, T], F32R)
        xT_lo = sb("xT_lo", [P, KC, T], F32R)

        ident = sb("ident", [P, P])
        wkT = sb("wkT", [CD + 1, CD])
        ctx_tok = sb("ctx_tok", [P, NT, KV, HD])
        rows = sb("rows", [P, 2 * D + E + 4])
        gamma, beta = rows[:, 0:D], rows[:, D:2 * D]
        router_bias = rows[:, 2 * D:2 * D + E]
        router = sb("router", [P, 2, KC, E])
        router_hi = sb("router_hi", [P, 2, KC, E], F32R)
        router_lo = sb("router_lo", [P, 2, KC, E], F32R)
        tanh_g = sb("tanh_g", [P, 4])
        half_pow = sb("half_pow", [P, NT])

        x = sb("x", [P, NT, D])
        xn = sb("xn", [P, NT, D])
        bn = sb("bn", [P, NT, 6])
        mv = sb("mv", [P, NT, 2])
        var = sb("var", [P, NT])
        rstd = sb("rstd", [P, NT])

        neg_max = sb("neg_max", [P, NT])
        exp_sum = sb("exp_sum", [P, NT])
        coef = sb("coef", [P, NT])

        w_raw = sb("w_raw", [P, 2, W0])
        w_hi = sb("w_hi", [P, 2, W0], F32R)
        w_lo = sb("w_lo", [P, 2, 3 * D], F32R)
        nonlin = sb("nonlin", [P, 2, HALF])
        gated = sb("gated", [P, HALF])
        act = sb("act", [P, HALF])
        act_hi = sb("act_hi", [P, 2, HALF], F32R)
        act_lo = sb("act_lo", [P, 2, HALF], F32R)
        cwT = sb("cwT", [P, T], F32R)

        logit = sb("logit", [P, NT, E + 4])
        mark = sb("mark", [P, NT, E + 4])
        top8 = sb("top8", [P, NT, 8])
        take = sb("take", [P, NT, 8])
        score = sb("score", [P, NT, E])
        chosen = sb("chosen", [P, NT, E])
        pair = sb("pair", [P, 6, NT * GROUPS])
        gsum = sb("gsum", [P, NT, GROUPS + 4])
        gmark = sb("gmark", [P, NT, GROUPS + 4])
        gtake = sb("gtake", [P, NT, 8])
        wsum = sb("wsum", [P, NT])
        cw = sb("cw", [P, NT, GW])
        cw_split = sb("cw_split", [P, NT, 2 * GW])

        k_tok = sb("k_tok", [P, 2, KV, G, 32])
        kS = sb("kS", [P, KV, T], F32R)
        vw = sb("vw", [P, NT, KV, 2 * WIN + QW])
        row_max = sb("row_max", [P, NT, KV, G])
        neg_mT = sb("neg_mT", [NH, NB, S], F32R)
        oq = sb("oq", [QW * QH, 2, S])
        o_rec = sb("o_rec", [P, 2, QH])
        o_tok = sb("o_tok", [P, 2, QH, HD])

        ctx_in, ctxtok_in, ident_in, rows_in = sem("ctx_in"), sem("ctxtok_in"), sem("ident_in"), sem("rows_in")
        x_in = [sem("x_in0"), sem("x_in1")]
        w_in = [[sem("w0_in0"), sem("w0_in1")], [sem("w1_in0"), sem("w1_in1")]]
        mrow_in = sem("mrow_in")
        out_done = sem("out_done")
        chain = sem("chain")
        pool_chain = sem("pool_chain")
        ctx_split = sem("ctx_split")
        router_split = sem("router_split")
        consts_set = sem("consts_set")
        vw_set = sem("vw_set")
        tanh_done = sem("tanh_done")
        kv_ready, kv_saved = sem("kv_ready"), sem("kv_saved")
        ktok_ready, kT_ready, kT_saved = sem("ktok_ready"), sem("kT_ready"), sem("kT_saved")
        var_ready, rstd_ready, xn_ready = sem("var_ready"), sem("rstd_ready"), sem("xn_ready")
        xnT_ready, xnT_saved = sem("xnT_ready"), sem("xnT_saved")
        outT_ready, outT_saved = sem("outT_ready"), sem("outT_saved")
        sim_ready, simvar_ready, simr_ready = sem("sim_ready"), sem("simvar_ready"), sem("simr_ready")
        z_ready, e_ready = sem("z_ready"), sem("e_ready")
        xT_ready, xhi_ready, xlo_ready = sem("xT_ready"), sem("xhi_ready"), sem("xlo_ready")
        logits_ready, lmax_ready, lexp_ready = sem("logits_ready"), sem("lmax_ready"), sem("lexp_ready")
        cw_ready, cwT_ready, cwT_saved = sem("cw_ready"), sem("cwT_ready"), sem("cwT_saved")

        def two(name):
            return [sem(name + "0"), sem(name + "1")]

        whi_done, wlo_done = two("whi_done"), two("wlo_done")
        gate_ready, cwb_ready, up_ready = two("gate_ready"), two("cwb_ready"), two("up_ready")
        nonlin_done, gated_done, act_done = two("nonlin_done"), two("gated_done"), two("act_done")
        acthi_done, actlo_done, down_done = two("acthi_done"), two("actlo_done"), two("down_done")
        qtok_ready, qT_ready, qT_saved = sem("qtok_ready"), sem("qT_ready"), sem("qT_saved")
        s_ready, max_done = sem("s_ready"), sem("max_done")
        mT_ready, mT_saved = sem("mT_ready"), sem("mT_saved")
        st_ready, exp_done, av_step = sem("st_ready"), sem("exp_done"), sem("av_step")
        oq_saved, ot_ready, ot_read, o_added = sem("oq_saved"), sem("ot_ready"), sem("ot_read"), sem("o_added")
        x_done = [sem("x_done_A"), sem("x_done_B"), sem("x_done_D")]

        NCH = [NC0, NC1]
        WCOL = [W0, W1]
        SU = 32
        STEPS = 16

        def s_units(k):
            return range(min(3 * k, SU), min(3 * k + 3, SU))

        M_STEP = 12

        block = ctx.enter_context(nc.Block())

        @block.sync
        def _(sp):
            sp.dma_start(ctxT[:], ctxT_d).then_inc(ctx_in, 16)
            sp.dma_start(wkT[:], wkT_d).then_inc(ctx_in, 16)
            xt = x_d.rearrange("b (s p) d -> p (b s) d", p=P)
            sp.dma_start(x[:, 4:8], xt[:, 4:8]).then_inc(x_in[1], 16)
            sp.dma_start(rows[:], rows_d).then_inc(rows_in, 16)
            sp.dma_start(router[:], router_d).then_inc(rows_in, 16)

            def load(stage, c, slot):
                src = (w0_d, w1_d)[stage]
                sp.dma_start(w_raw[:, slot, 0:WCOL[stage]], src[c]).then_inc(w_in[stage][slot], 16)

            def first_loads(stage):
                for slot in range(2):
                    if stage:
                        sp.wait_ge(wlo_done[0], NC0 - 1 + slot)
                    load(stage, slot, slot)

            def other_loads(stage):
                with sp.Fori(1, NCH[stage] // 2) as i:
                    for slot in range(2):
                        sp.wait_ge(wlo_done[stage], 2 * i + (slot - 1))
                        load(stage, 2 * i + slot, slot)

            first_loads(0)
            other_loads(0)
            first_loads(1)
            for b in range(NB):
                sp.wait_ge(mT_saved, b + 1)
                for g in range(G):
                    sp.dma_start(qS[32 * g + 24:32 * g + 25, :, b * S:(b + 1) * S].bitcast(F32),
                                 neg_mT[g:NH:G, b, :].bitcast(F32)).then_inc(mrow_in, 16)
            other_loads(1)
            ot = out_d.rearrange("b (s p) d -> p (b s) d", p=P)
            for q in range(4):
                sp.wait_ge(x_done[2], q + 1)
                sp.dma_start(ot[:, 2 * q:2 * q + 2], x[:, 2 * q:2 * q + 2]).then_inc(out_done, 16)
            sp.wait_ge(out_done, 64)

        @block.gpsimd
        def _(pool):
            pool.memset(half_pow[:], -0.5).then_inc(pool_chain, 1)
            pool.wait_ge(pool_chain, 1)

            def ln_rstd(stage):
                for h in range(2):
                    pool.wait_ge(var_ready, 2 * stage + h + 1)
                    pool.tensor_tensor(rstd[:, 4 * h:4 * h + 4], var[:, 4 * h:4 * h + 4],
                                       half_pow[:, 0:4], ALU.pow).then_inc(rstd_ready, 1)

            def w_low(stage, c, slot):
                n = WCOL[stage] - P
                pool.wait_ge(whi_done[stage], c + 1)
                pool.tensor_tensor(w_lo[:, slot, 0:n], w_raw[:, slot, 0:n],
                                   w_hi[:, slot, 0:n].bitcast(F32), ALU.subtract).then_inc(wlo_done[stage], 1)

            ln_rstd(0)
            pool.memset(vw[:, 0:4], 0.0).then_inc(pool_chain, 1)
            for b in range(NB):
                pool.wait_ge(simvar_ready, b + 1)
                pool.tensor_tensor(rstd[:, 2 * b:2 * b + 2], var[:, 2 * b:2 * b + 2],
                                   half_pow[:, 0:2], ALU.pow).then_inc(simr_ready, 1)
            w_low(0, 0, 0)
            pool.memset(vw[:, 4:8], 0.0).then_inc(pool_chain, 1)
            ln_rstd(1)
            pool.wait_ge(ctxtok_in, 16)
            pool.wait_ge(pool_chain, 3)
            for n in range(NT):
                pool.tensor_copy(vw[:, n, :, WIN:WIN + HD], ctx_tok[:, n]).then_inc(vw_set, 1)
            pool.memset(vw[:, :, :, WIN + HD:WIN + QW], 1.0).then_inc(vw_set, 1)
            w_low(0, 1, 1)
            with pool.Fori(1, NC0 // 2) as i:
                for slot in range(2):
                    w_low(0, 2 * i + slot, slot)
            ln_rstd(2)
            w_low(1, 0, 0)
            ln_rstd(3)
            w_low(1, 1, 1)
            with pool.Fori(1, NC1 // 2) as i:
                for slot in range(2):
                    w_low(1, 2 * i + slot, slot)

        @block.scalar
        def _(sc):
            xt = x_d.rearrange("b (s p) d -> p (b s) d", p=P)
            sc.dma_start(x[:, 0:4], xt[:, 0:4]).then_inc(x_in[0], 16)
            sc.dma_start(ctx_tok[:], ctx_d.rearrange("b (s p) (j d) -> p (b s) j d", p=P, d=HD)).then_inc(ctxtok_in, 16)
            sc.dma_start(ident[:], ident_d).then_inc(ident_in, 16)

            def k_split(n):
                if n == 0:
                    sc.wait_ge(ctx_split, 2)
                    sc.wait_ge(consts_set, 2)
                if n >= 2:
                    sc.wait_ge(kT_ready, 2 * (n - 1))
                for part, src in ((0, ctx_hi), (1, ctx_hi), (2, ctx_lo)):
                    sc.activation(k_tok[:, n % 2, :, :, 8 * part:8 * part + 8],
                                  src[:, n].bitcast(F32).unsqueeze(2).broadcast_to([P, KV, G, HD]),
                                  ACT.Copy).then_inc(ktok_ready, 1)

            def k_save(n):
                for jh in range(2):
                    sc.wait_ge(kT_ready, 2 * n + jh + 1)
                    sc.activation(kS[:, 4 * jh:4 * jh + 4, n * P:(n + 1) * P],
                                  bank[5 + jh].rearrange("p (j t) -> p j t", j=4), ACT.Copy).then_inc(kT_saved, 1)

            sc.wait_ge(kv_ready, 3)
            sc.activation(kv[:].rearrange("p n c -> p (n c)"), bank[2], ACT.Copy).then_inc(kv_saved, 1)
            for h in range(2):
                sc.activation(kvT[:, h * HALF:(h + 1) * HALF], bank[h][0:CD, :], ACT.Copy).then_inc(kv_saved, 1)
            for n in range(NT // 2):
                k_split(n)
                if n:
                    k_save(n - 1)
            k_save(NT // 2 - 1)
            for b in range(NB):
                sc.wait_ge(xnT_ready, b + 1)
                sc.activation(xnT[:, b].rearrange("p k s -> p (k s)"), bank[3 + b % 2], ACT.Copy).then_inc(xnT_saved, 1)
                if b:
                    sc.wait_ge(outT_ready, b)
                    sc.activation(outT[:, b - 1], bank[7][0:CD, 0:S], ACT.Copy).then_inc(outT_saved, 1)
            sc.wait_ge(outT_ready, NB)
            sc.activation(outT[:, NB - 1], bank[7][0:CD, 0:S], ACT.Copy).then_inc(outT_saved, 1)
            sc.wait_ge(rows_in, 32)
            sc.activation(tanh_g[:], rows[:, 2 * D + E:2 * D + E + 4], ACT.Tanh).then_inc(tanh_done, 1)
            for n in range(NT // 2, NT):
                k_split(n)
                if n > NT // 2:
                    k_save(n - 1)
            k_save(NT - 1)
            for n in range(NT):
                sc.wait_ge(z_ready, n // 2 + 1)
                sc.activation(xn[:, n], xn[:, n], ACT.Exp, bias=neg_max[:, n:n + 1],
                              accum_out=exp_sum[:, n:n + 1]).then_inc(e_ready, 1)

            def w_high(stage, c, slot):
                n = WCOL[stage]
                sc.wait_ge(w_in[stage][slot], 8 * (c - slot) + 16)
                sc.activation(w_hi[:, slot, 0:n], w_raw[:, slot, 0:n], ACT.Copy).then_inc(whi_done[stage], 1)

            def x_high(stage):
                for u in range(4):
                    h, k = u // 2, u % 2
                    sc.wait_ge(xT_ready, 4 * stage + u + 1)
                    sc.activation(xT_hi[:, k, h * HALF:(h + 1) * HALF], bank[4 + u], ACT.Copy).then_inc(xhi_ready, 1)

            def experts(stage):
                def one(c, slot, last=False):
                    for h in range(2):
                        blk = 2 * c + h
                        sc.wait_ge(gate_ready[stage], blk + 1)
                        if not (isinstance(c, int) and c == 0):
                            sc.wait_ge(gated_done[stage], blk - 1)
                            if stage:
                                sc.wait_ge(act_done[stage], blk - 1)
                        src = bank[0] if stage == 0 else bank[h]
                        sc.activation(nonlin[:, h], src, ACT.Relu if stage else ACT.Silu).then_inc(nonlin_done[stage], 1)
                        if h == 0 and not last:
                            if not (isinstance(c, int) and c == 0):
                                sc.wait_ge(down_done[stage], 2 * c)
                            w_high(stage, c + 1, 1 - slot)

                one(0, 0)
                one(1, 1)
                with sc.Fori(1, NCH[stage] // 2 - 1) as i:
                    one(2 * i, 0)
                    one(2 * i + 1, 1)
                one(NCH[stage] - 2, 0)
                one(NCH[stage] - 1, 1, last=True)

            def route(stage):
                sc.wait_ge(lmax_ready, stage + 1)
                sc.activation(score[:], score[:], ACT.Exp, scale=-1.0 if stage else 1.0).then_inc(lexp_ready, 1)
                for h in range(2):
                    sc.wait_ge(cwT_ready, 2 * stage + h + 1)
                    sc.activation(cwT[:, h * HALF:(h + 1) * HALF], bank[3 - h], ACT.Copy).then_inc(cwT_saved, 1)

            w_high(0, 0, 0)
            x_high(0)
            route(0)
            experts(0)

            sc.wait_ge(down_done[0], 2 * NC0)
            w_high(1, 0, 0)
            for u in range(2 * NT):
                n, jh = u // 2, u % 2
                sc.wait_ge(qT_ready, u + 1)
                sc.activation(qS[:, 4 * jh:4 * jh + 4, n * P:(n + 1) * P],
                              bank[4 + u % 4].rearrange("p (j t) -> p j t", j=4), ACT.Copy).then_inc(qT_saved, 1)

            def save_oq(qi):
                sc.wait_ge(av_step, 4 * (qi + 1))
                if qi >= 2:
                    sc.wait_ge(ot_ready, qi - 1)
                sc.activation(oq[:, qi % 2], bank[6 + qi % 2][0:QW * QH, 0:S], ACT.Copy).then_inc(oq_saved, 1)

            for step in range(NB * STEPS):
                sc.wait_ge(st_ready, step + 1)
                if step >= 2:
                    sc.wait_ge(av_step, step - 1)
                sc.activation(ex[:, step % 2], psum[:, 4:6, :].rearrange("p g (j s) -> p g j s", j=2), ACT.Exp,
                              scale=SCORE_SCALE).then_inc(exp_done, 1)
                if step % 4 == 1 and step > 4:
                    save_oq(step // 4 - 1)
            save_oq(4 * NB - 1)

            x_high(1)
            route(1)
            experts(1)

        @block.tensor
        def _(pe):
            def flip(out, src, inc=None):
                n = src.shape[0]
                ins = pe.transpose(out, src, ident[0:n, 0:n])
                if inc is not None:
                    ins.then_inc(inc, 1)

            pe.wait_ge(ctx_in, 32)
            for h in range(2):
                pe.matmul(bank[h][0:CD, :], wkT[:], ctxT[:, h * HALF:(h + 1) * HALF],
                          start=True, stop=True).then_inc(kv_ready, 1)
            for n in range(NT):
                last = pe.matmul(bank[2][:, n * CD:(n + 1) * CD], ctxT[:, n * P:(n + 1) * P], wkT[:],
                                 start=True, stop=True)
            last.then_inc(kv_ready, 1)
            pe.wait_ge(ident_in, 16)

            def k_flip(n):
                pe.wait_ge(ktok_ready, 3 * (n + 1))
                for jh in range(2):
                    if n:
                        pe.wait_ge(kT_saved, 2 * n + jh - 1)
                    for jj in range(4):
                        src = k_tok[:, n % 2, 4 * jh + jj].rearrange("p g c -> p (g c)")
                        flip(bank[5 + jh][:, jj * P:(jj + 1) * P], src, kT_ready if jj == 3 else None)

            def xn_flip(b):
                pe.wait_ge(xn_ready, 2 * b + 2)
                if b >= 2:
                    pe.wait_ge(xnT_saved, b - 1)
                for k in range(KC):
                    for st in range(2):
                        u = 2 * k + st
                        flip(bank[3 + b % 2][:, u * P:(u + 1) * P], xn[:, 2 * b + st, k * P:(k + 1) * P],
                             xnT_ready if u == 3 else None)

            def out_mm(b):
                pe.wait_ge(xnT_saved, b + 1)
                pe.wait_ge(kv_saved, 3)
                if b:
                    pe.wait_ge(outT_saved, b)
                for k in range(KC):
                    last = pe.matmul(bank[7][0:CD, 0:S], kv[:, 2 * b + k], xnT[:, b, k],
                                     start=(k == 0), stop=(k == KC - 1))
                last.then_inc(outT_ready, 1)

            def sim_mm(b):
                pe.wait_ge(outT_saved, b + 1)
                for st in range(2):
                    last = pe.matmul(bank[b][:, st * S:(st + 1) * S], outT[:, b, st * P:(st + 1) * P],
                                     kvT[:, b * S:(b + 1) * S], start=True, stop=True)
                last.then_inc(sim_ready, 1)

            for n in range(NT // 2):
                k_flip(n)
            xn_flip(0)
            xn_flip(1)
            for b in range(NB):
                out_mm(b)
                if b + 2 < NB:
                    xn_flip(b + 2)
                sim_mm(b)
            for n in range(NT // 2, NT):
                k_flip(n)
            pe.wait_ge(kT_saved, 2 * NT)

            def x_flip(stage):
                for u in range(4):
                    h, k = u // 2, u % 2
                    pe.wait_ge(xn_ready, (2 * stage + 1) * NT + 4 * h + 4)
                    for tt in range(4):
                        flip(bank[4 + u][:, tt * P:(tt + 1) * P], xn[:, 4 * h + tt, k * P:(k + 1) * P],
                             xT_ready if tt == 3 else None)
                pe.wait_ge(router_split, 2)
                for n in range(NT):
                    pe.wait_ge(xlo_ready, 4 * stage + 2 * (n // 4) + 2)
                    m = 0
                    for xp, rp in ((xT_hi, router_hi), (xT_hi, router_lo), (xT_lo, router_hi)):
                        for k in range(KC):
                            last = pe.matmul(bank[3][:, n * E:(n + 1) * E], xp[:, k, n * P:(n + 1) * P],
                                             rp[:, stage, k, :], start=(m == 0), stop=(m == 5))
                            m += 1
                last.then_inc(logits_ready, 1)

            def experts(stage):
                sel = WCOL[stage] - P

                def inner(out, col, slot, h, done):
                    m = 0
                    for wp, xp in ((w_hi, xT_hi), (w_hi, xT_lo), (w_lo, xT_hi)):
                        for k in range(KC):
                            last = pe.matmul(out, wp[:, slot, col + k * P:col + (k + 1) * P],
                                             xp[:, k, h * HALF:(h + 1) * HALF], start=(m == 0), stop=(m == 5))
                            m += 1
                    last.then_inc(done[stage], 1)

                def weights_per_token(slot, h):
                    pe.matmul(bank[2], w_hi[:, slot, sel:sel + P], cwT[:, h * HALF:(h + 1) * HALF],
                              start=True, stop=True).then_inc(cwb_ready[stage], 1)

                def down(blk, slot, h, first=False, final=False):
                    pe.wait_ge(actlo_done[stage], blk + 1)
                    for tt in range(4):
                        n = 4 * h + tt
                        m = 0
                        for ap, wp in ((act_hi, w_hi), (act_hi, w_lo), (act_lo, w_hi)):
                            last = pe.matmul(bank[4 + n // 2][:, (n % 2) * D:(n % 2 + 1) * D],
                                             ap[:, h, tt * P:(tt + 1) * P], wp[:, slot, 0:D],
                                             start=first and n % 2 == 0 and m == 0, stop=final and m == 2,
                                             skip_group_check=True)
                            m += 1
                    last.then_inc(down_done[stage], 1)

                def chunk(c, slot, first=False):
                    for h in range(2):
                        blk = 2 * c + h
                        if h == 0:
                            pe.wait_ge(whi_done[stage], c + 1)
                            pe.wait_ge(wlo_done[stage], c + 1)
                        if stage == 0:
                            if not (first and h == 0):
                                pe.wait_ge(nonlin_done[stage], blk)
                            inner(bank[0], D, slot, h, gate_ready)
                        else:
                            if not first:
                                pe.wait_ge(nonlin_done[stage], blk - 1)
                            inner(bank[h], D, slot, h, gate_ready)
                        if first and h == 0:
                            if stage == 0:
                                inner(bank[1], 2 * D, slot, h, up_ready)
                            for hh in range(2):
                                pe.wait_ge(cw_ready, stage + 1)
                                for tt in range(4):
                                    flip(bank[3 - hh][:, tt * P:(tt + 1) * P], cw_split[:, 4 * hh + tt],
                                         cwT_ready if tt == 3 else None)
                            pe.wait_ge(cwT_saved, 2 * stage + 2)
                            weights_per_token(slot, h)
                            continue
                        pe.wait_ge(gated_done[stage], blk)
                        weights_per_token(slot, h)
                        if stage == 0:
                            pe.wait_ge(act_done[stage], blk)
                            inner(bank[1], 2 * D, slot, h, up_ready)
                        down(blk - 1, slot if h else 1 - slot, 1 - h, first=first or (first is None and h == 0))

                chunk(0, 0, first=True)
                chunk(1, 1, first=None)
                with pe.Fori(1, NCH[stage] // 2) as i:
                    chunk(2 * i, 0)
                    chunk(2 * i + 1, 1)
                down(2 * NCH[stage] - 1, 1, 1, final=True)

            x_flip(0)
            experts(0)

            for u in range(2 * NT):
                n, jh = u // 2, u % 2
                pe.wait_ge(qtok_ready, 3 * (n + 1))
                if u >= 4:
                    pe.wait_ge(qT_saved, u - 3)
                for jj in range(4):
                    src = q_tok[:, n % 2, 4 * jh + jj].rearrange("p g c -> p (g c)")
                    flip(bank[4 + u % 4][:, jj * P:(jj + 1) * P], src, qT_ready if jj == 3 else None)

            def s_mm(b, su):
                st, jp, g = su // 16, su // 4 % 4, su % 4
                gs = SU * b + su
                pe.wait_ge(qT_saved, 2 * (2 * b + st + 1))
                if gs >= 3:
                    pe.wait_ge(max_done, gs - 2)
                for jj in range(2):
                    j = 2 * jp + jj
                    last = pe.matmul(bank[gs % 3][:, jj * S:(jj + 1) * S],
                                     qS[32 * g:32 * g + 32, j, (2 * b + st) * P:(2 * b + st + 1) * P],
                                     kS[32 * g:32 * g + 32, j, b * S:(b + 1) * S], start=True, stop=True)
                last.then_inc(s_ready, 1)

            def max_flip(b, quarters):
                pe.wait_ge(max_done, SU * (b + 1))
                if quarters:
                    pe.wait_ge(ot_read, quarters)
                for st in range(2):
                    flip(bank[3][0:NH, st * P:(st + 1) * P], row_max[:, 2 * b + st].rearrange("p j g -> p (j g)"),
                         mT_ready if st == 1 else None)

            def st_mm(b, k):
                q, gp, tc = k // 4, k // 2 % 2, k % 2
                step = STEPS * b + k
                if k == 0:
                    pe.wait_ge(mrow_in, 64 * (b + 1))
                if step:
                    pe.wait_ge(exp_done, step)
                for jj in range(2):
                    for gi in range(2):
                        g, j = 2 * gp + gi, 2 * q + jj
                        last = pe.matmul(bank[4 + gi][:, jj * S:(jj + 1) * S],
                                         kS[32 * g:32 * g + 32, j, b * S + tc * P:b * S + (tc + 1) * P],
                                         qS[32 * g:32 * g + 32, j, b * S:(b + 1) * S], start=True, stop=True)
                last.then_inc(st_ready, 1)

            def av_mm(b, k):
                q, gp, tc = k // 4, k // 2 % 2, k % 2
                step, qi = STEPS * b + k, 4 * b + q
                pe.wait_ge(exp_done, step + 1)
                if k % 4 == 0 and qi >= 2:
                    pe.wait_ge(oq_saved, qi - 1)
                for gi in range(2):
                    for jj in range(2):
                        i = 4 * jj + 2 * gp + gi
                        at = WIN - QW * i
                        last = pe.matmul(bank[6 + qi % 2][0:QW * QH, 0:S],
                                         vw[:, 2 * b + tc, 2 * q + jj, at:at + QW * QH],
                                         ex[:, step % 2, gi, jj, :],
                                         start=(k % 4 == 0 and gi == 0 and jj == 0),
                                         stop=(k % 4 == 3 and gi == 1 and jj == 1))
                last.then_inc(av_step, 1)

            def o_flip(qi, maxima):
                pe.wait_ge(oq_saved, qi + 1)
                if qi:
                    pe.wait_ge(ot_read, qi)
                pe.wait_ge(mT_saved, maxima)
                for st in range(2):
                    flip_to = bank[3][:, st * QW * QH:(st + 1) * QW * QH]
                    flip(flip_to, oq[:, qi % 2, st * P:(st + 1) * P], ot_ready if st == 1 else None)

            for su in range(SU):
                s_mm(0, su)
            max_flip(0, 0)
            pe.wait_ge(qT_saved, 2 * NT)
            pe.wait_ge(vw_set, NT + 1)
            for b in range(NB):
                for k in range(STEPS):
                    step = STEPS * b + k
                    st_mm(b, k)
                    if step:
                        av_mm((step - 1) // STEPS, (step - 1) % STEPS)
                    if b + 1 < NB:
                        for su in s_units(k):
                            s_mm(b + 1, su)
                        if k == M_STEP:
                            max_flip(b + 1, (step - 2) // 4)
                    if step % 4 == 2 and step > 4:
                        o_flip(step // 4 - 1, min(b + 1 + (k > M_STEP), NB))
            av_mm(NB - 1, STEPS - 1)
            o_flip(4 * NB - 1, NB)

            x_flip(1)
            experts(1)

        @block.vector
        def _(ve):
            steps = [0]

            def step(ins):
                ins.then_inc(chain, 1)
                steps[0] += 1

            def settled():
                ve.wait_ge(chain, steps[0])

            def over(ap, shape):
                return ap.broadcast_to(shape)

            ve.memset(k_tok[:, :, :, :, 24:32], 0.0).then_inc(consts_set, 1)
            ve.wait_ge(consts_set, 1)
            ve.memset(k_tok[:, :, :, :, 24:25], 1.0).then_inc(consts_set, 1)
            ve.wait_ge(ctxtok_in, 16)
            ve.tensor_copy(ctx_hi[:], ctx_tok[:]).then_inc(ctx_split, 1)
            ve.wait_ge(ctx_split, 1)
            ve.tensor_tensor(ctx_lo[:], ctx_tok[:], ctx_hi[:].bitcast(F32), ALU.subtract).then_inc(ctx_split, 1)

            def ln(stage):
                for h in range(2):
                    if stage == 0:
                        ve.wait_ge(x_in[h], 16)
                    for n in range(4 * h, 4 * h + 4):
                        step(ve.bn_stats(bn[:, n], x[:, n]))
                    settled()
                    for n in range(4 * h, 4 * h + 4):
                        step(ve.bn_aggr(mv[:, n], bn[:, n]))
                    settled()
                    ve.tensor_scalar_add(var[:, 4 * h:4 * h + 4], mv[:, 4 * h:4 * h + 4, 1], LN_EPS).then_inc(var_ready, 1)
                for h in range(2):
                    ve.wait_ge(rstd_ready, 2 * stage + h + 1)
                    for n in range(4 * h, 4 * h + 4):
                        ve.tensor_scalar(xn[:, n], x[:, n], mv[:, n, 0:1], rstd[:, n:n + 1],
                                         ALU.subtract, ALU.mult).then_inc(xn_ready, 1)

            ln(0)
            step(ve.memset(logit[:, :, E:], SENT))
            step(ve.memset(gsum[:, :, GROUPS:], SENT))
            step(ve.memset(take[:], SENT))
            step(ve.memset(gtake[:], SENT))
            step(ve.memset(cw[:], 0.0))
            ve.wait_ge(rows_in, 32)
            ve.tensor_copy(router_hi[:], router[:]).then_inc(router_split, 1)
            ve.wait_ge(router_split, 1)
            ve.tensor_tensor(router_lo[:], router[:], router_hi[:].bitcast(F32), ALU.subtract).then_inc(router_split, 1)
            for b in range(NB):
                ve.wait_ge(sim_ready, b + 1)
                for st in range(2):
                    step(ve.bn_stats(bn[:, 2 * b + st], bank[b][:, st * S:(st + 1) * S]))
                settled()
                for st in range(2):
                    step(ve.bn_aggr(mv[:, 2 * b + st], bn[:, 2 * b + st]))
                settled()
                ve.tensor_scalar_add(var[:, 2 * b:2 * b + 2], mv[:, 2 * b:2 * b + 2, 1],
                                     SIM_EPS / SIM_SCALE ** 2).then_inc(simvar_ready, 1)

            def sim_norm(b):
                ve.wait_ge(simr_ready, b + 1)
                for st in range(2):
                    n = 2 * b + st
                    step(ve.scalar_tensor_tensor(xn[:, n], bank[b][:, st * S:(st + 1) * S], mv[:, n, 0:1], gamma,
                                                 ALU.subtract, ALU.mult))
                settled()
                for st in range(2):
                    n = 2 * b + st
                    step(ve.scalar_tensor_tensor(xn[:, n], xn[:, n], rstd[:, n:n + 1], beta, ALU.mult, ALU.add))
                settled()
                step(ve.tensor_reduce(neg_max[:, 2 * b:2 * b + 2], xn[:, 2 * b:2 * b + 2], AX.X, ALU.max))
                settled()
                ve.tensor_scalar(neg_max[:, 2 * b:2 * b + 2], neg_max[:, 2 * b:2 * b + 2], -1.0, None,
                                 ALU.mult).then_inc(z_ready, 1)

            def sim_add(b):
                ve.wait_ge(e_ready, 2 * b + 2)
                ve.wait_ge(tanh_done, 1)
                step(ve.reciprocal(coef[:, 2 * b:2 * b + 2], exp_sum[:, 2 * b:2 * b + 2]))
                settled()
                step(ve.tensor_scalar(coef[:, 2 * b:2 * b + 2], coef[:, 2 * b:2 * b + 2], tanh_g[:, 0:1], None, ALU.mult))
                settled()
                for n in (2 * b, 2 * b + 1):
                    ve.scalar_tensor_tensor(x[:, n], xn[:, n], coef[:, n:n + 1], x[:, n],
                                            ALU.mult, ALU.add).then_inc(x_done[0], 1)

            sim_norm(0)
            for b in range(1, NB):
                sim_norm(b)
                sim_add(b - 1)
            sim_add(NB - 1)

            def x_low(stage):
                for u in range(4):
                    h, k = u // 2, u % 2
                    ve.wait_ge(xhi_ready, 4 * stage + u + 1)
                    ve.tensor_tensor(xT_lo[:, k, h * HALF:(h + 1) * HALF], bank[4 + u],
                                     xT_hi[:, k, h * HALF:(h + 1) * HALF].bitcast(F32), ALU.subtract).then_inc(xlo_ready, 1)

            def choose(values, taken, width, top, taker, out):
                for n in range(NT):
                    step(ve.max(top8[:, n], values[:, n, 0:width]))
                settled()
                step(ve.tensor_copy(taker[:, :, 0:top], top8[:, :, 0:top]))
                settled()
                for n in range(NT):
                    step(ve.match_replace(taken[:, n], taker[:, n], values[:, n], TAKEN))
                settled()
                step(ve.tensor_tensor(out, taken[:, :, 0:width], values[:, :, 0:width], ALU.not_equal))
                settled()

            def weigh(stage):
                step(ve.tensor_tensor(cw[:, :, 0:E], score[:], chosen[:], ALU.mult))
                settled()
                step(ve.tensor_reduce(wsum[:], cw[:, :, 0:E], AX.X, ALU.add))
                settled()
                if stage:
                    step(ve.tensor_scalar_add(wsum[:], wsum[:], 1e-20))
                    settled()
                step(ve.reciprocal(wsum[:], wsum[:]))
                settled()
                if stage:
                    step(ve.tensor_scalar(wsum[:], wsum[:], ROUTE_SCALE, None, ALU.mult))
                    settled()
                step(ve.tensor_tensor(cw[:, :, 0:E], cw[:, :, 0:E], over(wsum[:].unsqueeze(2), [P, NT, E]), ALU.mult))
                settled()

            def split_cw():
                step(ve.tensor_copy(cw_split[:, :, 0:GW].bitcast(F32R), cw[:]))
                settled()
                ve.tensor_tensor(cw_split[:, :, GW:2 * GW], cw[:], cw_split[:, :, 0:GW], ALU.subtract).then_inc(cw_ready, 1)

            def route_softmax():
                ve.wait_ge(logits_ready, 1)
                step(ve.tensor_copy(logit[:, :, 0:E], bank[3][:, 0:NT * E].rearrange("p (n e) -> p n e", e=E)))
                settled()
                step(ve.tensor_reduce(wsum[:], logit[:, :, 0:E], AX.X, ALU.max))
                settled()
                ve.tensor_tensor(score[:], logit[:, :, 0:E], over(wsum[:].unsqueeze(2), [P, NT, E]),
                                 ALU.subtract).then_inc(lmax_ready, 1)
                choose(logit, mark, E, TOP0, take, chosen[:])
                ve.wait_ge(lexp_ready, 1)
                weigh(0)
                small = cw[:, :, E:E + CHUNKS0]
                step(ve.tensor_tensor(small, cw[:, :, 0:E:2], cw[:, :, 1:E:2], ALU.add))
                settled()
                step(ve.tensor_scalar(small, small, SMALL_SCALE, None, ALU.mult))
                settled()
                split_cw()

            def route_sigmoid():
                ve.wait_ge(logits_ready, 2)
                ve.tensor_tensor(score[:], bank[3][:, 0:NT * E].rearrange("p (n e) -> p n e", e=E),
                                 over(router_bias.unsqueeze(1), [P, NT, E]), ALU.add).then_inc(lmax_ready, 1)
                ve.wait_ge(lexp_ready, 2)
                step(ve.tensor_scalar_add(score[:], score[:], 1.0))
                settled()
                step(ve.reciprocal(score[:], score[:]))
                settled()
                s4 = score[:].rearrange("p n (g e) -> p (n g) e", e=E // GROUPS)
                high0, low0, high1, low1, both, same = (pair[:, i] for i in range(6))
                step(ve.tensor_tensor(high0, s4[:, :, 0], s4[:, :, 1], ALU.max))
                step(ve.tensor_tensor(low0, s4[:, :, 0], s4[:, :, 1], ALU.min))
                step(ve.tensor_tensor(high1, s4[:, :, 2], s4[:, :, 3], ALU.max))
                step(ve.tensor_tensor(low1, s4[:, :, 2], s4[:, :, 3], ALU.min))
                settled()
                step(ve.tensor_tensor(both, high0, high1, ALU.add))
                step(ve.tensor_tensor(same, high0, low0, ALU.add))
                step(ve.tensor_tensor(low1, high1, low1, ALU.add))
                settled()
                step(ve.tensor_tensor(same, same, low1, ALU.max))
                settled()
                step(ve.tensor_tensor(gsum[:, :, 0:GROUPS], both.rearrange("p (n g) -> p n g", g=GROUPS),
                                      same.rearrange("p (n g) -> p n g", g=GROUPS), ALU.max))
                settled()
                in_group = pair[:, 0].rearrange("p (n g) -> p n g", g=GROUPS)
                choose(gsum, gmark, GROUPS, GTOP, gtake, in_group)
                step(ve.tensor_tensor(logit[:, :, 0:E].rearrange("p n (g e) -> p n g e", g=GROUPS),
                                      score[:].rearrange("p n (g e) -> p n g e", g=GROUPS),
                                      over(in_group.unsqueeze(3), [P, NT, GROUPS, E // GROUPS]), ALU.mult))
                step(ve.memset(cw[:, :, E:GW], 0.0))
                settled()
                step(ve.memset(cw[:, :, E:NC1], 1.0))
                choose(logit, mark, E, TOP1, take, chosen[:])
                weigh(1)
                split_cw()

            def experts(stage):
                def chunk(c, first=False):
                    for h in range(2):
                        blk = 2 * c + h
                        ve.wait_ge(nonlin_done[stage], blk + 1)
                        ve.wait_ge(cwb_ready[stage], blk + 1)
                        ve.tensor_tensor(gated[:], nonlin[:, h], bank[2], ALU.mult).then_inc(gated_done[stage], 1)
                        ve.wait_ge(gated_done[stage], blk + 1)
                        if stage == 0:
                            ve.wait_ge(up_ready[stage], blk + 1)
                        ve.tensor_tensor(act[:], gated[:], nonlin[:, h] if stage else bank[1],
                                         ALU.mult).then_inc(act_done[stage], 1)
                        ve.wait_ge(act_done[stage], blk + 1)
                        if not first:
                            ve.wait_ge(down_done[stage], blk - 1)
                        ve.tensor_copy(act_hi[:, h], act[:]).then_inc(acthi_done[stage], 1)
                        ve.wait_ge(acthi_done[stage], blk + 1)
                        ve.tensor_tensor(act_lo[:, h], act[:], act_hi[:, h].bitcast(F32),
                                         ALU.subtract).then_inc(actlo_done[stage], 1)

                chunk(0, first=True)
                chunk(1)
                with ve.Fori(1, NCH[stage] // 2) as i:
                    chunk(2 * i)
                    chunk(2 * i + 1)
                for q in range(4):
                    ve.wait_ge(down_done[stage], 2 * NCH[stage] - 1 + q // 2)
                    xq = x[:, 2 * q:2 * q + 2].rearrange("p n d -> p (n d)")
                    ve.scalar_tensor_tensor(xq, bank[4 + q], tanh_g[:, 2 + stage:3 + stage], xq,
                                            ALU.mult, ALU.add).then_inc(x_done[1 + stage], 1)

            ve.wait_ge(x_done[0], NT)
            ln(1)
            x_low(0)
            route_softmax()
            experts(0)

            step(ve.memset(q_tok[:, :, :, :, 24:32], 0.0))
            ve.wait_ge(x_done[1], 4)
            ln(2)
            for n in range(NT):
                q8 = xn[:, n].rearrange("p (j g d) -> p j g d", g=G, d=HD)
                buf = q_tok[:, n % 2]
                ve.wait_ge(xn_ready, 2 * NT + n + 1)
                if n >= 2:
                    ve.wait_ge(qT_ready, 2 * (n - 1))
                ve.tensor_copy(buf[:, :, :, 0:8].bitcast(F32R), q8).then_inc(qtok_ready, 1)
                ve.wait_ge(qtok_ready, 3 * n + 1)
                ve.tensor_tensor(buf[:, :, :, 8:16], q8, buf[:, :, :, 0:8], ALU.subtract).then_inc(qtok_ready, 1)
                ve.tensor_copy(buf[:, :, :, 16:24], buf[:, :, :, 0:8]).then_inc(qtok_ready, 1)

            def unit_max(b, su):
                st, jp, g = su // 16, su // 4 % 4, su % 4
                gs = SU * b + su
                ve.wait_ge(s_ready, gs + 1)
                ve.tensor_reduce(row_max[:, 2 * b + st, 2 * jp:2 * jp + 2, g],
                                 bank[gs % 3].rearrange("p (j t) -> p j t", j=2), AX.X, ALU.max).then_inc(max_done, 1)

            def save_max(b):
                ve.wait_ge(mT_ready, b + 1)
                ve.tensor_scalar(neg_mT[:, b], bank[3][0:NH, 0:S], -1.0, None, ALU.mult).then_inc(mT_saved, 1)

            def add_o(qi):
                b, q = qi // 4, qi % 4
                ve.wait_ge(ot_ready, qi + 1)
                ot = bank[3][:, 0:2 * QH * QW].rearrange("p (s i c) -> p s i c", s=2, c=QW)
                step(ve.reciprocal(o_rec[:], ot[:, :, :, HD]))
                settled()
                ve.tensor_tensor(o_tok[:], ot[:, :, :, 0:HD], over(o_rec[:].unsqueeze(3), [P, 2, QH, HD]),
                                 ALU.mult).then_inc(ot_read, 1)
                ve.wait_ge(ot_read, qi + 1)
                xs = x[:, 2 * b:2 * b + 2, q * QH * HD:(q + 1) * QH * HD]
                ve.scalar_tensor_tensor(xs, o_tok[:].rearrange("p s i d -> p s (i d)"), tanh_g[:, 1:2], xs,
                                        ALU.mult, ALU.add).then_inc(o_added, 1)

            for su in range(SU):
                unit_max(0, su)
            save_max(0)
            for b in range(NB):
                for k in range(STEPS):
                    st = STEPS * b + k
                    if b + 1 < NB:
                        for su in s_units(k):
                            unit_max(b + 1, su)
                        if k == M_STEP:
                            save_max(b + 1)
                    if st % 4 == 2 and st > 4:
                        add_o(st // 4 - 1)
            add_o(4 * NB - 1)

            ve.wait_ge(o_added, 4 * NB)
            ln(3)
            x_low(1)
            route_sigmoid()
            experts(1)


def _layouts(v):
    f = np.float32

    def split_rows(w):
        return w.reshape(KC, P, -1).transpose(1, 0, 2)

    def inner_first(w):
        return w.transpose(1, 0, 2).reshape(D, -1)

    def chunks(up, n):
        return up.reshape(KC, P, n, P).transpose(2, 1, 0, 3).reshape(n, P, KC * P)

    gate = np.concatenate([inner_first(v["L0_ffn_Wg"]), inner_first(v["L0_ffn_cWg"])], 1)
    up = np.concatenate([inner_first(v["L0_ffn_Wu"]), inner_first(v["L0_ffn_cWu"])], 1)
    down = np.concatenate([v["L0_ffn_Wd"].reshape(-1, D), v["L0_ffn_cWd"].reshape(-1, D)], 0)
    unit = np.arange(NC0 * P)
    big = E * INTER0
    expert = np.where(unit < big, unit // INTER0, E + (unit - big) // P).reshape(NC0, 1, P)
    sel0 = (np.arange(P).reshape(1, P, 1) % GW == expert).astype(f)
    w0 = np.concatenate([down.reshape(NC0, P, D), chunks(gate, NC0), chunks(up, NC0), sel0], 2)

    up1 = np.concatenate([v["L1_ffn_W1"].reshape(-1, D), v["L1_ffn_Ws1"]], 0).T
    down1 = np.concatenate([v["L1_ffn_W2"].transpose(0, 2, 1).reshape(-1, D), v["L1_ffn_Ws2"].T], 0)
    sel1 = (np.arange(P).reshape(1, P, 1) % GW == np.arange(NC1).reshape(NC1, 1, 1)).astype(f)
    w1 = np.concatenate([down1.reshape(NC1, P, D), chunks(up1, NC1), np.broadcast_to(sel1, (NC1, P, P))], 2)

    ctx = v["ctx_512"].reshape(T, CD)
    row = np.concatenate([v["L0_xattn_ln_gamma"], v["L0_xattn_ln_beta"], v["L1_ffn_br"], v["g_xattn"], v["g_ffn"]])
    router = np.stack([split_rows(v["L0_ffn_gate_w"].T), split_rows(v["L1_ffn_Wr"].T)], 1)
    return {
        "x": v["x"],
        "ctx": v["ctx_512"],
        "ctxT": np.concatenate([ctx.T, np.ones((1, T), f)], 0),
        "wkT": np.concatenate([v["L0_xattn_W_k"].T, v["L0_xattn_b_k"][None]], 0),
        "rows": np.broadcast_to(row, (P, row.size)),
        "router": router,
        "ident": np.eye(P, dtype=f),
        "w0": w0,
        "w1": w1,
    }


def kernel(**inputs):
    import concourse.bacc as bacc
    from concourse.bass_utils import run_bass_kernel_spmd

    laid = _layouts({k: np.asarray(a) for k, a in inputs.items()})
    nc = bacc.Bacc("TRN2", target_bir_lowering=False, num_devices=1)
    arrays, args = {}, []
    for name, a in laid.items():
        a = np.ascontiguousarray(a)
        arrays[f"in_{name}"] = a
        args.append(nc.dram_tensor(f"in_{name}", a.shape, mybir.dt.from_np(a.dtype), kind="ExternalInput").ap())
    args.append(nc.dram_tensor("out_x", (NB, S, D), F32, kind="ExternalOutput").ap())
    build(nc, *args)
    r = run_bass_kernel_spmd(nc, [arrays], core_ids=[0])
    return r.results[0]["out_x"]
```

```python
from contextlib import ExitStack

import numpy as np

import concourse.bass as bass
from concourse import mybir

ALU = mybir.AluOpType
ACT = mybir.ActivationFunctionType
AX = mybir.AxisListType
F32 = mybir.dt.float32
F32R = mybir.dt.float32r

P = 128
NB = 4
S = 256
T = NB * S
NT = T // P
HALF = 512
D = 256
KC = D // P
CD = 64
HD = 8
KV = CD // HD
G = D // HD // KV
NH = KV * G
E = 32
TOP0, TOP1, GROUPS, GTOP = 4, 6, 8, 4
INTER0, CHUNKS0 = 96, 16
SMALL_SCALE = 0.05
ROUTE_SCALE = 2.5
NC0 = E * INTER0 // P + CHUNKS0
NC1 = D // P + E
W0 = 3 * D
W1 = 2 * D
SHARED = D // P
SEG = 32
NSEG = NC0 * P // SEG
GW = E + CHUNKS0
SENT = 3.0e38
TAKEN = -3.0e38
LN_EPS = 1e-5
SIM_EPS = 1e-6
SIM_SCALE = 1.0 / 16.0
QW = 9
QH = 8
WIN = QW * (QH - 1)
SCORE_SCALE = HD ** -0.5


def build(nc, x_d, ctx_d, ctxT_d, wkT_d, rows_d, router_d, ident_d, select_d, w0_d, w1_d, out_d, cw0_d, cw1_d):
    with ExitStack() as ctx:
        def sb(name, shape, dt=F32):
            return ctx.enter_context(nc.sbuf_tensor(name, shape, dt))

        def sem(name):
            return ctx.enter_context(nc.semaphore(name))

        psum = ctx.enter_context(nc.psum_tensor("psum", [P, 8, 512], F32))
        bank = [psum[:, i, :] for i in range(8)]

        with ExitStack() as scope:
            def early(name, shape, dt=F32):
                return scope.enter_context(nc.sbuf_tensor(name, shape, dt))

            ctxT = early("ctxT", [CD + 1, T])
            ctx_tok = early("ctx_tok", [P, NT, KV, HD])
            kv = early("kv", [P, NT, CD])
            kvT = early("kvT", [CD, T])
            xnT = early("xnT", [P, NB, KC, S])
            outT = early("outT", [CD, NB, S])
        qS = sb("qS", [P, KV, T], F32R)
        with ExitStack() as scope:
            vw_hi = scope.enter_context(nc.sbuf_tensor("vw_hi", [P, 2, 2, KV, 2 * WIN + QW], F32R))
            vw_lo = scope.enter_context(nc.sbuf_tensor("vw_lo", [P, 2, 2, KV, 2 * WIN + QW], F32R))
        w_hi = sb("w_hi", [P, 2, W0], F32R)
        w_lo = sb("w_lo", [P, 2, W0], F32R)
        cwB = sb("cwB", [P, 2, T])
        nonlin = sb("nonlin", [P, 2, HALF])
        product = sb("product", [P, 2, HALF])
        act_hi = sb("act_hi", [P, 2, HALF], F32R)
        act_lo = sb("act_lo", [P, 2, HALF], F32R)
        w_raw = sb("w_raw", [P, 2, W0])

        ident = sb("ident", [P, P])
        select = sb("select", [GW, 2, P])
        wkT = sb("wkT", [CD + 1, CD])
        ctx_hi = sb("ctx_hi", [P, NT, KV, HD], F32R)
        ctx_lo = sb("ctx_lo", [P, NT, KV, HD], F32R)
        rows = sb("rows", [P, 2 * D + E + 4])
        gamma, beta = rows[:, 0:D], rows[:, D:2 * D]
        router_bias = rows[:, 2 * D:2 * D + E]
        router = sb("router", [P, 2, KC, E])
        router_hi = sb("router_hi", [P, 2, KC, E], F32R)
        router_lo = sb("router_lo", [P, 2, KC, E], F32R)
        tanh_g = sb("tanh_g", [P, 4])
        half_pow = sb("half_pow", [P, NT])

        x = sb("x", [P, NT, D])
        xn = sb("xn", [P, NT, D])
        xT_hi = sb("xT_hi", [P, KC, T], F32R)
        xT_lo = sb("xT_lo", [P, KC, T], F32R)
        bn = sb("bn", [P, NT, 6])
        mv = sb("mv", [P, NT, 2])
        var = sb("var", [P, NT])
        rstd = sb("rstd", [P, NT])
        neg_max = sb("neg_max", [P, NT])
        exp_sum = sb("exp_sum", [P, NT])
        coef = sb("coef", [P, NT])

        logit = sb("logit", [P, NT, E + 4])
        mark = sb("mark", [P, NT, E + 4])
        top8 = sb("top8", [P, NT, 8])
        take = sb("take", [P, NT, 8])
        score = sb("score", [P, NT, E])
        chosen = sb("chosen", [P, NT, E])
        pair = sb("pair", [P, 6, NT * GROUPS])
        gsum = sb("gsum", [P, NT, GROUPS + 4])
        gmark = sb("gmark", [P, NT, GROUPS + 4])
        gtake = sb("gtake", [P, NT, 8])
        wsum = sb("wsum", [P, NT])
        cw = sb("cw", [P, NT, GW])
        cwT = sb("cwT", [GW, T])

        k_tok = sb("k_tok", [P, 2, KV, G, 32])
        q_tok = k_tok
        kS = sb("kS", [P, KV, T], F32R)
        row_max = sb("row_max", [P, NT, KV, G])
        neg_mT = sb("neg_mT", [QH, 2, S], F32R)
        ex = sb("ex", [P, 2, 2, 2, S])
        ex_hi = sb("ex_hi", [P, 3, 2, 2, S], F32R)
        ex_lo = sb("ex_lo", [P, 3, 2, 2, S], F32R)
        oq = sb("oq", [QW * QH, 2, S])
        o_rec = sb("o_rec", [P, 2, QH])
        o_tok = sb("o_tok", [P, 2, QH, HD])

        ctx_in, ctxtok_in, ident_in, rows_in = sem("ctx_in"), sem("ctxtok_in"), sem("ident_in"), sem("rows_in")
        select_in = sem("select_in")
        x_in = [sem("x_in0"), sem("x_in1")]
        w_in = [[sem("w0_in0"), sem("w0_in1")], [sem("w1_in0"), sem("w1_in1")]]
        mrow_in = sem("mrow_in")
        out_done = sem("out_done")
        chain = sem("chain")
        pool_chain = sem("pool_chain")
        ctx_split = sem("ctx_split")
        router_split = sem("router_split")
        consts_set = sem("consts_set")
        vw_set = sem("vw_set")
        tanh_done = sem("tanh_done")
        kv_ready, kv_saved = sem("kv_ready"), sem("kv_saved")
        ktok_ready, kT_ready, kT_saved = sem("ktok_ready"), sem("kT_ready"), sem("kT_saved")
        var_ready, rstd_ready, xn_ready = sem("var_ready"), sem("rstd_ready"), sem("xn_ready")
        xnT_ready, xnT_saved = sem("xnT_ready"), sem("xnT_saved")
        outT_ready, outT_saved = sem("outT_ready"), sem("outT_saved")
        sim_ready, simvar_ready, simr_ready = sem("sim_ready"), sem("simvar_ready"), sem("simr_ready")
        z_ready, e_ready = sem("z_ready"), sem("e_ready")
        xT_ready, xhi_ready, xlo_ready = sem("xT_ready"), sem("xhi_ready"), sem("xlo_ready")
        logits_ready, lmax_ready, lexp_ready = sem("logits_ready"), sem("lmax_ready"), sem("lexp_ready")
        cw_ready, cwT_ready, cwT_saved = sem("cw_ready"), sem("cwT_ready"), sem("cwT_saved")
        cw_written = [sem("cw_written0"), sem("cw_written1")]
        cw_in = [[sem("cw0_in0"), sem("cw0_in1")], [sem("cw1_in0"), sem("cw1_in1")]]
        lgT_ready, lgT_saved = sem("lgT_ready"), sem("lgT_saved")
        cwu_ready = sem("cwu_ready")
        relu_done = sem("relu_done")
        exp_loaded = sem("exp_loaded")

        def two(name):
            return [sem(name + "0"), sem(name + "1")]

        whi_done, wlo_done = two("whi_done"), two("wlo_done")
        gate_ready, up_ready = two("gate_ready"), two("up_ready")
        nonlin_done, gated_done, act_done = two("nonlin_done"), two("gated_done"), two("act_done")
        acthi_done, actlo_done, down_done = two("acthi_done"), two("actlo_done"), two("down_done")
        qtok_ready, qT_ready, qT_saved = sem("qtok_ready"), sem("qT_ready"), sem("qT_saved")
        s_ready, max_done = sem("s_ready"), sem("max_done")
        mT_ready, mT_saved = sem("mT_ready"), sem("mT_saved")
        exhi_done, exlo_done, exlo2_done = sem("exhi_done"), sem("exlo_done"), sem("exlo2_done")
        st_ready, exp_done, av_step = sem("st_ready"), sem("exp_done"), sem("av_step")
        oq_saved, ot_ready, ot_read, o_added = sem("oq_saved"), sem("ot_ready"), sem("ot_read"), sem("o_added")
        x_done = [sem("x_done_A"), sem("x_done_B"), sem("x_done_D")]

        NCH = [NC0, NC1]
        WCOL = [W0, W1]
        XBANK = [[0, 1, 4, 5], [0, 1, 6, 7]]
        LTBANK = [(3, 7), (0, 1)]
        CWB = [(5, 7), (2, 3)]
        CWU = [(4, 6), (2, 3)]
        CW_FIRST = [0, SHARED]
        STEPS = 16
        NSTEP = NB * STEPS
        K_STATS, K_APPLY, K_SPLIT0, K_SPLIT1 = 6, 8, 13, 1
        QFLIP = {15: (2, 0), 0: (1, 1), 3: (1, 2), 4: (1, 3)}
        D_STATS, D_APPLY, D_FLIP, D_LOGITS, D_STATS2, D_APPLY2 = 8, 9, 11, 13, 12, 13

        block = ctx.enter_context(nc.Block())

        @block.sync
        def _(sp):
            sp.dma_start(ctxT[:], ctxT_d).then_inc(ctx_in, 16)
            sp.dma_start(wkT[:], wkT_d).then_inc(ctx_in, 16)
            xt = x_d.rearrange("b (s p) d -> p (b s) d", p=P)
            sp.dma_start(x[:, 4:8], xt[:, 4:8]).then_inc(x_in[1], 16)
            sp.dma_start(rows[:], rows_d).then_inc(rows_in, 16)
            sp.dma_start(router[:], router_d).then_inc(rows_in, 16)
            sp.dma_start(select[:], select_d).then_inc(select_in, 16)

            def load(stage, c, slot):
                src = (w0_d, w1_d)[stage]
                sp.dma_start(w_raw[:, slot, 0:WCOL[stage]], src[c]).then_inc(w_in[stage][slot], 16)

            def load_cw(stage, c, slot):
                if stage == 0:
                    for s in range(P // SEG):
                        row = cw0_d[bass.ds(c * (P // SEG) + s, 1), :]
                        sp.dma_start(cwB[s * SEG:(s + 1) * SEG, slot, :],
                                     row.broadcast_to([SEG, T])).then_inc(cw_in[0][slot], 16)
                else:
                    row = cw1_d[bass.ds(c - SHARED, 1), :]
                    sp.dma_start(cwB[:, slot, :], row.broadcast_to([P, T])).then_inc(cw_in[1][slot], 16)

            def first_loads(stage):
                for slot in range(2):
                    if stage:
                        sp.wait_ge(wlo_done[0], NC0 - 1 + slot)
                    load(stage, slot, slot)

            def next_load(stage, c, slot, cw=True):
                sp.wait_ge(wlo_done[stage], c - 1)
                load(stage, c, slot)
                if cw:
                    sp.wait_ge((gated_done[0], act_done[1])[stage], 2 * c - 2)
                    load_cw(stage, c, slot)

            def other_loads(stage, first):
                with sp.Fori(first, NCH[stage] // 2) as i:
                    for slot in range(2):
                        sp.wait_ge(wlo_done[stage], 2 * i + (slot - 1))
                        load(stage, 2 * i + slot, slot)
                        sp.wait_ge((gated_done[0], act_done[1])[stage], 4 * i + (2 * slot - 2))
                        load_cw(stage, 2 * i + slot, slot)

            first_loads(0)
            sp.wait_ge(cw_written[0], 64)
            load_cw(0, 1, 1)
            other_loads(0, 1)
            first_loads(1)
            for mq in range(4 * NB):
                b, q = mq // 4, mq % 4
                sp.wait_ge(mT_saved, mq + 1)
                for g in range(G):
                    sp.dma_start(qS[32 * g + 24:32 * g + 25, 2 * q:2 * q + 2, b * S:(b + 1) * S].bitcast(F32),
                                 neg_mT[g:QH:G, mq % 2, :].bitcast(F32)).then_inc(mrow_in, 16)
            next_load(1, 2, 0, cw=False)
            sp.wait_ge(cw_written[1], 32)
            next_load(1, 3, 1)
            other_loads(1, 2)
            ot = out_d.rearrange("b (s p) d -> p (b s) d", p=P)
            for q in range(4):
                sp.wait_ge(x_done[2], q + 1)
                sp.dma_start(ot[:, 2 * q:2 * q + 2], x[:, 2 * q:2 * q + 2]).then_inc(out_done, 16)
            sp.wait_ge(out_done, 64)

        @block.gpsimd
        def _(pool):
            pool.memset(half_pow[:], -0.5).then_inc(pool_chain, 1)
            pool.wait_ge(pool_chain, 1)

            def ln_rstd(group, tiles):
                pool.wait_ge(var_ready, group + 1)
                a, b = tiles[0], tiles[-1] + 1
                pool.tensor_tensor(rstd[:, a:b], var[:, a:b], half_pow[:, 0:b - a], ALU.pow).then_inc(rstd_ready, 1)

            def w_low(stage, c, slot):
                n = WCOL[stage]
                pool.wait_ge(whi_done[stage], c + 1)
                pool.tensor_tensor(w_lo[:, slot, 0:n], w_raw[:, slot, 0:n],
                                   w_hi[:, slot, 0:n].bitcast(F32), ALU.subtract).then_inc(wlo_done[stage], 1)

            for h in range(2):
                ln_rstd(h, range(4 * h, 4 * h + 4))

            def sim_rstd(b):
                pool.wait_ge(simvar_ready, b + 1)
                pool.tensor_tensor(rstd[:, 2 * b:2 * b + 2], var[:, 2 * b:2 * b + 2],
                                   half_pow[:, 0:2], ALU.pow).then_inc(simr_ready, 1)

            for b in range(NB):
                sim_rstd(b)
            w_low(0, 0, 0)
            for b in range(NB):
                ln_rstd(2 + b, (2 * b, 2 * b + 1))
            w_low(0, 1, 1)
            with pool.Fori(1, NC0 // 2) as i:
                for slot in range(2):
                    w_low(0, 2 * i + slot, slot)

            ln_rstd(6, (0, 1))
            pool.wait_ge(down_done[0], 2 * NC0)
            pool.memset(vw_hi[:].bitcast(F32), 0.0).then_inc(pool_chain, 1)
            ln_rstd(7, (2, 3))
            pool.memset(vw_lo[:].bitcast(F32), 0.0).then_inc(pool_chain, 1)
            pool.wait_ge(pool_chain, 3)
            pool.memset(vw_hi[:, :, :, :, WIN + HD:WIN + QW].bitcast(F32), 1.0).then_inc(vw_set, 1)

            def values(b):
                if b >= 2:
                    pool.wait_ge(av_step, STEPS * (b - 1))
                for tc in range(2):
                    for vw, part in ((vw_hi, ctx_hi), (vw_lo, ctx_lo)):
                        pool.tensor_copy(vw[:, b % 2, tc, :, WIN:WIN + HD],
                                         part[:, 2 * b + tc].bitcast(F32)).then_inc(vw_set, 1)

            values(0)
            for step in range(NSTEP):
                b, k = step // STEPS, step % STEPS
                if k == K_STATS and b + 2 < NB:
                    ln_rstd(8 + b, (2 * b + 4, 2 * b + 5))
                if b == NB - 1 and k == D_STATS:
                    ln_rstd(10, range(4))
                if b == NB - 1 and k == D_STATS2:
                    ln_rstd(11, (4, 5))
                if k == 4 and b + 1 < NB:
                    values(b + 1)
                pool.wait_ge(exhi_done, step + 1)
                if step >= 3:
                    pool.wait_ge(av_step, step - 2)
                pool.tensor_tensor(ex_lo[:, step % 3, 1], ex[:, step % 2, 1],
                                   ex_hi[:, step % 3, 1].bitcast(F32), ALU.subtract).then_inc(exlo2_done, 1)
            ln_rstd(12, (6, 7))
            for c in range(2):
                w_low(1, c, c)
            with pool.Fori(1, NC1 // 2) as i:
                for slot in range(2):
                    w_low(1, 2 * i + slot, slot)

        @block.scalar
        def _(sc):
            xt = x_d.rearrange("b (s p) d -> p (b s) d", p=P)
            sc.dma_start(x[:, 0:4], xt[:, 0:4]).then_inc(x_in[0], 16)
            sc.dma_start(ctx_tok[:], ctx_d.rearrange("b (s p) (j d) -> p (b s) j d", p=P, d=HD)).then_inc(ctxtok_in, 16)
            sc.dma_start(ident[:], ident_d).then_inc(ident_in, 16)

            def k_split(n):
                if n == 0:
                    sc.wait_ge(ctx_split, 2)
                    sc.wait_ge(consts_set, 2)
                if n >= 2:
                    sc.wait_ge(kT_ready, 2 * (n - 1))
                for part, src in ((0, ctx_hi), (1, ctx_hi), (2, ctx_lo)):
                    sc.activation(k_tok[:, n % 2, :, :, 8 * part:8 * part + 8],
                                  src[:, n].bitcast(F32).unsqueeze(2).broadcast_to([P, KV, G, HD]),
                                  ACT.Copy).then_inc(ktok_ready, 1)

            def k_save(n):
                for jh in range(2):
                    sc.wait_ge(kT_ready, 2 * n + jh + 1)
                    sc.activation(kS[:, 4 * jh:4 * jh + 4, n * P:(n + 1) * P],
                                  bank[5 + jh].rearrange("p (j t) -> p j t", j=4), ACT.Copy).then_inc(kT_saved, 1)

            sc.wait_ge(kv_ready, 3)
            sc.activation(kv[:].rearrange("p n c -> p (n c)"), bank[2], ACT.Copy).then_inc(kv_saved, 1)
            for h in range(2):
                sc.activation(kvT[:, h * HALF:(h + 1) * HALF], bank[h][0:CD, :], ACT.Copy).then_inc(kv_saved, 1)
            for b in range(NB + 1):
                if b < NB:
                    sc.wait_ge(xnT_ready, b + 1)
                    sc.activation(xnT[:, b].rearrange("p k s -> p (k s)"), bank[3 + b % 2],
                                  ACT.Copy).then_inc(xnT_saved, 1)
                if b:
                    sc.wait_ge(outT_ready, b)
                    sc.activation(outT[:, b - 1], bank[7][0:CD, 0:S], ACT.Copy).then_inc(outT_saved, 1)
                    k_split(b - 1)
                if b >= 2:
                    k_save(b - 2)
            k_save(NB - 1)
            sc.wait_ge(rows_in, 32)
            sc.activation(tanh_g[:], rows[:, 2 * D + E:2 * D + E + 4], ACT.Tanh).then_inc(tanh_done, 1)

            def w_high(stage, c, slot):
                n = WCOL[stage]
                sc.wait_ge(w_in[stage][slot], 8 * (c - slot) + 16)
                sc.activation(w_hi[:, slot, 0:n], w_raw[:, slot, 0:n], ACT.Copy).then_inc(whi_done[stage], 1)

            def x_high(stage, h):
                for k in range(KC):
                    u = 2 * h + k
                    sc.wait_ge(xT_ready, 4 * stage + u + 1)
                    sc.activation(xT_hi[:, k, h * HALF:(h + 1) * HALF], bank[XBANK[stage][u]], ACT.Copy).then_inc(xhi_ready, 1)

            def save_logits(stage, h):
                sc.wait_ge(lgT_ready, 2 * stage + h + 1)
                sc.activation(cwT[0:E, h * HALF:(h + 1) * HALF], bank[LTBANK[stage][h]][0:E, :],
                              ACT.Copy).then_inc(lgT_saved, 1)

            def experts(stage):
                def one(c, slot, first=False, last=False):
                    for h in range(2):
                        blk = 2 * c + h
                        sc.wait_ge(gate_ready[stage], blk + 1)
                        if not first:
                            sc.wait_ge(act_done[stage], blk - 1)
                        if stage == 0:
                            sc.activation(nonlin[:, h], bank[2 * h], ACT.Silu).then_inc(nonlin_done[0], 1)
                        else:
                            sc.activation(nonlin[:, h], bank[h], ACT.Relu).then_inc(relu_done, 1)
                            sc.wait_ge(relu_done, blk + 1)
                            sc.activation(nonlin[:, h], nonlin[:, h], ACT.Square).then_inc(nonlin_done[1], 1)
                        if first and stage and h == 0:
                            x_high(1, 1)
                            save_logits(1, 1)
                            route_exp(1)
                        if h == 0 and not last:
                            if not first:
                                sc.wait_ge(down_done[stage], 2 * c)
                            w_high(stage, c + 1, 1 - slot)

                one(0, 0, first=True)
                if stage == 0:
                    save_cw(0)
                one(1, 1)
                if stage:
                    save_cw(1)
                with sc.Fori(1, NCH[stage] // 2 - 1) as i:
                    one(2 * i, 0)
                    one(2 * i + 1, 1)
                one(NCH[stage] - 2, 0)
                one(NCH[stage] - 1, 1, last=True)

            def save_cw(stage):
                for h in range(2):
                    sc.wait_ge(cwT_ready, 2 * stage + h + 1)
                    sc.activation(cwT[:, h * HALF:(h + 1) * HALF], bank[CWB[stage][h]][0:GW, :],
                                  ACT.Copy).then_inc(cwT_saved, 1)
                for h in range(2):
                    sc.wait_ge(cwT_saved, 2 * stage + h + 1)
                    half = slice(h * HALF, (h + 1) * HALF)
                    if stage:
                        sc.dma_start(cw1_d[:, half], cwT[0:E, half]).then_inc(cw_written[1], 16)
                        continue
                    big = INTER0 // SEG
                    small = P // SEG
                    sc.dma_start(cw0_d[0:E * big, half].rearrange("(e r) t -> e r t", r=big),
                                 cwT[0:E, half].unsqueeze(1).broadcast_to([E, big, HALF])).then_inc(cw_written[0], 16)
                    sc.dma_start(cw0_d[E * big:NSEG, half].rearrange("(e r) t -> e r t", r=small),
                                 cwT[E:GW, half].unsqueeze(1).broadcast_to([CHUNKS0, small, HALF]))\
                        .then_inc(cw_written[0], 16)

            def route_exp(stage):
                sc.wait_ge(lmax_ready, stage + 1)
                sc.activation(score[:], score[:], ACT.Exp, scale=-1.0 if stage else 1.0).then_inc(lexp_ready, 1)

            w_high(0, 0, 0)
            for b in range(NB):
                sc.wait_ge(z_ready, b + 1)
                for n in (2 * b, 2 * b + 1):
                    sc.activation(xn[:, n], xn[:, n], ACT.Exp, bias=neg_max[:, n:n + 1],
                                  accum_out=exp_sum[:, n:n + 1]).then_inc(e_ready, 1)
                if b in (1, 2):
                    for n in (NT // 2 + 2 * b - 2, NT // 2 + 2 * b - 1):
                        k_split(n)
                        k_save(n)

            for h in range(2):
                x_high(0, h)
            for h in range(2):
                save_logits(0, h)
            route_exp(0)
            experts(0)

            def q_save(u):
                n, jh = u // 2, u % 2
                sc.wait_ge(qT_ready, u + 1)
                src = bank[4 + u] if u < 4 else bank[3]
                sc.activation(qS[:, 4 * jh:4 * jh + 4, n * P:(n + 1) * P],
                              src.rearrange("p (j t) -> p j t", j=4), ACT.Copy).then_inc(qT_saved, 1)

            def save_oq(qi):
                sc.wait_ge(av_step, 4 * (qi + 1))
                if qi >= 2:
                    sc.wait_ge(ot_ready, qi - 1)
                sc.activation(oq[:, qi % 2], bank[6 + qi % 2][0:QW * QH, 0:S], ACT.Copy).then_inc(oq_saved, 1)

            sc.activation(coef[:, 0:1], half_pow[:, 0:1], ACT.Exp).then_inc(exp_loaded, 1)
            for u in range(4):
                q_save(u)
            for step in range(NSTEP):
                b, k = step // STEPS, step % STEPS
                sc.wait_ge(st_ready, step + 1)
                if step >= 2:
                    sc.wait_ge(exlo_done, step - 1)
                    sc.wait_ge(exlo2_done, step - 1)
                sc.activation(ex[:, step % 2], psum[:, 4:6, :].rearrange("p g (j s) -> p g j s", j=2), ACT.Exp,
                              scale=SCORE_SCALE).then_inc(exp_done, 1)
                sc.wait_ge(exp_done, step + 1)
                if step >= 3:
                    sc.wait_ge(av_step, step - 2)
                sc.activation(ex_hi[:, step % 3], ex[:, step % 2], ACT.Copy).then_inc(exhi_done, 1)
                if step == 0:
                    q_save(4)
                if k in QFLIP and b + QFLIP[k][0] < NB:
                    q_save(4 * (b + QFLIP[k][0]) + QFLIP[k][1])
                if step % 4 == 1 and step > 4:
                    save_oq(step // 4 - 1)
                if b == NB - 1 and k == D_FLIP:
                    x_high(1, 0)
                if b == NB - 1 and k == D_LOGITS:
                    save_logits(1, 0)
            save_oq(4 * NB - 1)

            sc.wait_ge(av_step, NSTEP)
            w_high(1, 0, 0)
            experts(1)

        @block.tensor
        def _(pe):
            def flip(out, src, inc=None):
                n = src.shape[0]
                ins = pe.transpose(out, src, ident[0:n, 0:n])
                if inc is not None:
                    ins.then_inc(inc, 1)

            pe.wait_ge(ctx_in, 32)
            for h in range(2):
                pe.matmul(bank[h][0:CD, :], wkT[:], ctxT[:, h * HALF:(h + 1) * HALF],
                          start=True, stop=True).then_inc(kv_ready, 1)
            for n in range(NT):
                last = pe.matmul(bank[2][:, n * CD:(n + 1) * CD], ctxT[:, n * P:(n + 1) * P], wkT[:],
                                 start=True, stop=True)
            last.then_inc(kv_ready, 1)
            pe.wait_ge(ident_in, 16)

            def k_flip(n):
                pe.wait_ge(ktok_ready, 3 * (n + 1))
                for jh in range(2):
                    if n:
                        pe.wait_ge(kT_saved, 2 * n + jh - 1)
                    for jj in range(4):
                        src = k_tok[:, n % 2, 4 * jh + jj].rearrange("p g c -> p (g c)")
                        flip(bank[5 + jh][:, jj * P:(jj + 1) * P], src, kT_ready if jj == 3 else None)

            def xn_flip(b):
                pe.wait_ge(xn_ready, 2 * b + 2)
                if b >= 2:
                    pe.wait_ge(xnT_saved, b - 1)
                for k in range(KC):
                    for st in range(2):
                        u = 2 * k + st
                        flip(bank[3 + b % 2][:, u * P:(u + 1) * P], xn[:, 2 * b + st, k * P:(k + 1) * P],
                             xnT_ready if u == 3 else None)

            def out_mm(b):
                pe.wait_ge(xnT_saved, b + 1)
                pe.wait_ge(kv_saved, 3)
                if b:
                    pe.wait_ge(outT_saved, b)
                for k in range(KC):
                    last = pe.matmul(bank[7][0:CD, 0:S], kv[:, 2 * b + k], xnT[:, b, k],
                                     start=(k == 0), stop=(k == KC - 1))
                last.then_inc(outT_ready, 1)

            def sim_mm(b):
                pe.wait_ge(outT_saved, b + 1)
                for st in range(2):
                    last = pe.matmul(bank[b][:, st * S:(st + 1) * S], outT[:, b, st * P:(st + 1) * P],
                                     kvT[:, b * S:(b + 1) * S], start=True, stop=True)
                last.then_inc(sim_ready, 1)

            xn_flip(0)
            xn_flip(1)
            for b in range(NB):
                out_mm(b)
                if b + 2 < NB:
                    xn_flip(b + 2)
                sim_mm(b)
                k_flip(b)
            for n in range(NB, NT):
                k_flip(n)

            def x_flip(stage, h):
                for k in range(KC):
                    u = 2 * h + k
                    pe.wait_ge(xn_ready, (2 * stage + 1) * NT + 4 * h + 4)
                    if stage == 0:
                        pe.wait_ge(kT_saved, 2 * NT)
                    for tt in range(4):
                        flip(bank[XBANK[stage][u]][:, tt * P:(tt + 1) * P], xn[:, 4 * h + tt, k * P:(k + 1) * P],
                             xT_ready if tt == 3 else None)

            def logits(stage, h):
                pe.wait_ge(router_split, 2)
                pe.wait_ge(xlo_ready, 4 * stage + 2 * h + 2)
                m = 0
                for rp, xp in ((router_hi, xT_hi), (router_lo, xT_hi), (router_hi, xT_lo)):
                    for k in range(KC):
                        last = pe.matmul(bank[LTBANK[stage][h]][0:E, :], rp[:, stage, k, :],
                                         xp[:, k, h * HALF:(h + 1) * HALF], start=(m == 0), stop=(m == 5))
                        m += 1
                last.then_inc(lgT_ready, 1)

            def logits_flip(stage, h):
                pe.wait_ge(lgT_saved, 2 * stage + h + 1)
                for n in range(4 * h, 4 * h + 4):
                    flip(bank[2][:, n * E:(n + 1) * E], cwT[0:E, n * P:(n + 1) * P],
                         logits_ready if n % 4 == 3 else None)

            def experts(stage):
                def inner(out, col, slot, h, done):
                    m = 0
                    for wp, xp in ((w_hi, xT_hi), (w_hi, xT_lo), (w_lo, xT_hi)):
                        for k in range(KC):
                            last = pe.matmul(out, wp[:, slot, col + k * P:col + (k + 1) * P],
                                             xp[:, k, h * HALF:(h + 1) * HALF], start=(m == 0), stop=(m == 5))
                            m += 1
                    last.then_inc(done[stage], 1)

                def flip_cw():
                    pe.wait_ge(cw_ready, stage + 1)
                    for hh in range(2):
                        for tt in range(4):
                            flip(bank[CWB[stage][hh]][0:GW, tt * P:(tt + 1) * P], cw[:, 4 * hh + tt],
                                 cwT_ready if tt == 3 else None)

                def spread_cw(hh):
                    if hh == 0:
                        pe.wait_ge(select_in, 16)
                    pe.wait_ge(cwT_saved, 2 * stage + hh + 1)
                    pe.matmul(bank[CWU[stage][hh]], select[:, stage, :], cwT[:, hh * HALF:(hh + 1) * HALF],
                              start=True, stop=True).then_inc(cwu_ready, 1)

                def down(blk, slot, h, first=False, final=False):
                    pe.wait_ge(acthi_done[stage], blk + 1)
                    for m, (ap, wp) in enumerate(((act_hi, w_hi), (act_hi, w_lo), (act_lo, w_hi))):
                        if m == 2:
                            pe.wait_ge(actlo_done[stage], blk + 1)
                        for tt in range(4):
                            n = 4 * h + tt
                            last = pe.matmul(bank[4 + n // 2][:, (n % 2) * D:(n % 2 + 1) * D],
                                             ap[:, h, tt * P:(tt + 1) * P], wp[:, slot, 0:D],
                                             start=first and n % 2 == 0 and m == 0, stop=final and m == 2,
                                             skip_group_check=True)
                    last.then_inc(down_done[stage], 1)

                def block_in(c, slot, h, first, after_first=False):
                    blk = 2 * c + h
                    if h == 0:
                        pe.wait_ge(whi_done[stage], c + 1)
                        pe.wait_ge(wlo_done[stage], c + 1)
                    if not first:
                        if stage == 0:
                            pe.wait_ge(nonlin_done[0], blk - 1)
                            pe.wait_ge((act_done if after_first else gated_done)[0], blk - 1)
                        else:
                            pe.wait_ge(relu_done, blk - 1)
                    if stage:
                        inner(bank[h], D, slot, h, gate_ready)
                    else:
                        inner(bank[2 * h], D, slot, h, gate_ready)
                        inner(bank[2 * h + 1], 2 * D, slot, h, up_ready)

                def chunk(c, slot):
                    for h in range(2):
                        block_in(c, slot, h, False)
                        down(2 * c + h - 1, slot if h else 1 - slot, 1 - h)

                if stage == 0:
                    block_in(0, 0, 0, True)
                    pe.wait_ge(lmax_ready, 1)
                    block_in(0, 0, 1, True)
                    flip_cw()
                    spread_cw(0)
                    spread_cw(1)
                    down(0, 0, 0, first=True)
                    block_in(1, 1, 0, False, after_first=True)
                    down(1, 0, 1, first=True)
                    block_in(1, 1, 1, False, after_first=True)
                    down(2, 1, 0)
                else:
                    block_in(0, 0, 0, True)
                    x_flip(1, 1)
                    logits(1, 1)
                    down(0, 0, 0, first=True)
                    logits_flip(1, 1)
                    block_in(0, 0, 1, True)
                    block_in(1, 1, 0, False)
                    down(1, 0, 1, first=True)
                    block_in(1, 1, 1, False)
                    down(2, 1, 0)
                    pe.wait_ge(lmax_ready, 2)
                    flip_cw()
                    spread_cw(0)
                    spread_cw(1)
                with pe.Fori(1, NCH[stage] // 2) as i:
                    chunk(2 * i, 0)
                    chunk(2 * i + 1, 1)
                down(2 * NCH[stage] - 1, 1, 1, final=True)

            for h in range(2):
                x_flip(0, h)
            for h in range(2):
                logits(0, h)
            for h in range(2):
                logits_flip(0, h)
            experts(0)

            flips = {"q": 0, "m": 0, "o": 0}

            def bank3_free():
                pe.wait_ge(qT_saved, flips["q"])
                if flips["m"]:
                    pe.wait_ge(mT_saved, flips["m"])
                if flips["o"]:
                    pe.wait_ge(ot_read, flips["o"])

            def q_flip(u):
                n, jh = u // 2, u % 2
                pe.wait_ge(qtok_ready, 3 * (n + 1))
                if u >= 4:
                    bank3_free()
                for jj in range(4):
                    src = q_tok[:, n % 2, 4 * jh + jj].rearrange("p g c -> p (g c)")
                    to = bank[4 + u] if u < 4 else bank[3]
                    flip(to[:, jj * P:(jj + 1) * P], src, qT_ready if jj == 3 else None)
                flips["q"] += 1

            def s_mm(gs):
                b, jp, st, g = gs // 32, gs // 8 % 4, gs // 4 % 2, gs % 4
                pe.wait_ge(qT_saved, 2 * (2 * b + st + 1))
                if gs >= 3:
                    pe.wait_ge(max_done, gs - 2)
                for jj in range(2):
                    j = 2 * jp + jj
                    last = pe.matmul(bank[gs % 3][:, jj * S:(jj + 1) * S],
                                     qS[32 * g:32 * g + 32, j, (2 * b + st) * P:(2 * b + st + 1) * P],
                                     kS[32 * g:32 * g + 32, j, b * S:(b + 1) * S], start=True, stop=True)
                last.then_inc(s_ready, 1)

            def max_flip(mq):
                b, q = mq // 4, mq % 4
                pe.wait_ge(max_done, 8 * (mq + 1))
                bank3_free()
                for st in range(2):
                    flip(bank[3][0:QH, st * P:(st + 1) * P],
                         row_max[:, 2 * b + st, 2 * q:2 * q + 2].rearrange("p j g -> p (j g)"),
                         mT_ready if st == 1 else None)
                flips["m"] += 1

            def st_mm(step):
                b, q, gp, tc = step // STEPS, step // 4 % 4, step // 2 % 2, step % 2
                if step % 4 == 0:
                    pe.wait_ge(mrow_in, 64 * (step // 4 + 1))
                if step:
                    pe.wait_ge(exp_done, step)
                for jj in range(2):
                    for gi in range(2):
                        g, j = 2 * gp + gi, 2 * q + jj
                        last = pe.matmul(bank[4 + gi][:, jj * S:(jj + 1) * S],
                                         kS[32 * g:32 * g + 32, j, b * S + tc * P:b * S + (tc + 1) * P],
                                         qS[32 * g:32 * g + 32, j, b * S:(b + 1) * S], start=True, stop=True)
                last.then_inc(st_ready, 1)

            def av_mm(step):
                b, q, gp, tc = step // STEPS, step // 4 % 4, step // 2 % 2, step % 2
                qi = step // 4
                pe.wait_ge(exlo_done, step + 1)
                pe.wait_ge(exlo2_done, step + 1)
                if step % STEPS == 0:
                    pe.wait_ge(vw_set, 4 * b + 5)
                if step % 4 == 0 and qi >= 2:
                    pe.wait_ge(oq_saved, qi - 1)
                m = 0
                for gi in range(2):
                    for jj in range(2):
                        at = WIN - QW * (4 * jj + 2 * gp + gi)
                        for vp, ep in ((vw_hi, ex_hi), (vw_lo, ex_hi), (vw_hi, ex_lo)):
                            last = pe.matmul(bank[6 + qi % 2][0:QW * QH, 0:S],
                                             vp[:, b % 2, tc, 2 * q + jj, at:at + QW * QH],
                                             ep[:, step % 3, gi, jj, :],
                                             start=(step % 4 == 0 and m == 0), stop=(step % 4 == 3 and m == 11))
                            m += 1
                last.then_inc(av_step, 1)

            def o_flip(qi):
                pe.wait_ge(oq_saved, qi + 1)
                bank3_free()
                for st in range(2):
                    flip(bank[3][:, st * QW * QH:(st + 1) * QW * QH], oq[:, qi % 2, st * P:(st + 1) * P],
                         ot_ready if st == 1 else None)
                flips["o"] += 1

            for u in range(4):
                q_flip(u)
            for gs in range(8):
                s_mm(gs)
            max_flip(0)
            for gs in range(8, 16):
                s_mm(gs)
            for step in range(NSTEP):
                b, k = step // STEPS, step % STEPS
                st_mm(step)
                ahead = 8 * (step // 4 + 2) + 2 * (step % 4)
                if ahead < 32 * NB:
                    s_mm(ahead)
                    s_mm(ahead + 1)
                if step >= 2:
                    av_mm(step - 2)
                if step == 0:
                    q_flip(4)
                if k in QFLIP and b + QFLIP[k][0] < NB:
                    q_flip(4 * (b + QFLIP[k][0]) + QFLIP[k][1])
                if step % 4 == 1 and step // 4 + 1 < 4 * NB:
                    max_flip(step // 4 + 1)
                if step % 4 == 2 and step > 4:
                    o_flip(step // 4 - 1)
                if b == NB - 1 and k == D_FLIP:
                    x_flip(1, 0)
                if b == NB - 1 and k == D_LOGITS:
                    logits(1, 0)
                if b == NB - 1 and k == D_LOGITS + 1:
                    logits_flip(1, 0)
            av_mm(NSTEP - 2)
            av_mm(NSTEP - 1)
            o_flip(4 * NB - 1)

            experts(1)

        @block.vector
        def _(ve):
            steps = [0]

            def step(ins):
                ins.then_inc(chain, 1)
                steps[0] += 1

            def settled():
                ve.wait_ge(chain, steps[0])

            def over(ap, shape):
                return ap.broadcast_to(shape)

            ve.memset(k_tok[:, :, :, :, 24:32], 0.0).then_inc(consts_set, 1)
            ve.wait_ge(consts_set, 1)
            ve.memset(k_tok[:, :, :, :, 24:25], 1.0).then_inc(consts_set, 1)

            def ln_stats(tiles):
                for n in tiles:
                    step(ve.bn_stats(bn[:, n], x[:, n]))
                settled()
                for n in tiles:
                    step(ve.bn_aggr(mv[:, n], bn[:, n]))
                settled()
                a, b = tiles[0], tiles[-1] + 1
                ve.tensor_scalar_add(var[:, a:b], mv[:, a:b, 1], LN_EPS).then_inc(var_ready, 1)

            def ln_apply(group, tiles):
                ve.wait_ge(rstd_ready, group + 1)
                for n in tiles:
                    ve.tensor_scalar(xn[:, n], x[:, n], mv[:, n, 0:1], rstd[:, n:n + 1],
                                     ALU.subtract, ALU.mult).then_inc(xn_ready, 1)

            def pair_of(b):
                return (2 * b, 2 * b + 1)

            for h in range(2):
                ve.wait_ge(x_in[h], 16)
                ln_stats(range(4 * h, 4 * h + 4))
            for h in range(2):
                ln_apply(h, range(4 * h, 4 * h + 4))
            ve.wait_ge(ctxtok_in, 16)
            ve.tensor_copy(ctx_hi[:], ctx_tok[:]).then_inc(ctx_split, 1)
            ve.wait_ge(ctx_split, 1)
            ve.tensor_tensor(ctx_lo[:], ctx_tok[:], ctx_hi[:].bitcast(F32), ALU.subtract).then_inc(ctx_split, 1)
            step(ve.memset(logit[:, :, E:], SENT))
            step(ve.memset(gsum[:, :, GROUPS:], SENT))
            step(ve.memset(take[:], SENT))
            step(ve.memset(gtake[:], SENT))
            step(ve.memset(cw[:], 0.0))
            ve.wait_ge(rows_in, 32)
            ve.tensor_copy(router_hi[:], router[:]).then_inc(router_split, 1)
            ve.wait_ge(router_split, 1)
            ve.tensor_tensor(router_lo[:], router[:], router_hi[:].bitcast(F32), ALU.subtract).then_inc(router_split, 1)

            def sim_stats(b):
                ve.wait_ge(sim_ready, b + 1)
                for st in range(2):
                    step(ve.bn_stats(bn[:, 2 * b + st], bank[b][:, st * S:(st + 1) * S]))
                settled()
                for st in range(2):
                    step(ve.bn_aggr(mv[:, 2 * b + st], bn[:, 2 * b + st]))
                settled()
                ve.tensor_scalar_add(var[:, 2 * b:2 * b + 2], mv[:, 2 * b:2 * b + 2, 1],
                                     SIM_EPS / SIM_SCALE ** 2).then_inc(simvar_ready, 1)

            def sim_norm(b):
                ve.wait_ge(simr_ready, b + 1)
                for st in range(2):
                    n = 2 * b + st
                    step(ve.scalar_tensor_tensor(xn[:, n], bank[b][:, st * S:(st + 1) * S], mv[:, n, 0:1], gamma,
                                                 ALU.subtract, ALU.mult))
                settled()
                for st in range(2):
                    n = 2 * b + st
                    step(ve.scalar_tensor_tensor(xn[:, n], xn[:, n], rstd[:, n:n + 1], beta, ALU.mult, ALU.add))
                settled()
                step(ve.tensor_reduce(neg_max[:, 2 * b:2 * b + 2], xn[:, 2 * b:2 * b + 2], AX.X, ALU.max))
                settled()
                ve.tensor_scalar(neg_max[:, 2 * b:2 * b + 2], neg_max[:, 2 * b:2 * b + 2], -1.0, None,
                                 ALU.mult).then_inc(z_ready, 1)

            def sim_add(b):
                ve.wait_ge(e_ready, 2 * b + 2)
                ve.wait_ge(tanh_done, 1)
                step(ve.reciprocal(coef[:, 2 * b:2 * b + 2], exp_sum[:, 2 * b:2 * b + 2]))
                settled()
                step(ve.tensor_scalar(coef[:, 2 * b:2 * b + 2], coef[:, 2 * b:2 * b + 2], tanh_g[:, 0:1], None, ALU.mult))
                settled()
                for n in (2 * b, 2 * b + 1):
                    ve.scalar_tensor_tensor(x[:, n], xn[:, n], coef[:, n:n + 1], x[:, n],
                                            ALU.mult, ALU.add).then_inc(x_done[0], 1)

            def x_low(stage, h):
                for k in range(KC):
                    u = 2 * h + k
                    ve.wait_ge(xhi_ready, 4 * stage + u + 1)
                    ve.tensor_tensor(xT_lo[:, k, h * HALF:(h + 1) * HALF], bank[XBANK[stage][u]],
                                     xT_hi[:, k, h * HALF:(h + 1) * HALF].bitcast(F32), ALU.subtract).then_inc(xlo_ready, 1)

            sim_stats(0)
            sim_stats(1)
            sim_norm(0)
            sim_stats(2)
            sim_norm(1)
            sim_stats(3)
            for b in range(NB):
                sim_add(b)
                ve.wait_ge(x_done[0], 2 * b + 2)
                ln_stats(pair_of(b))
                if b + 2 < NB:
                    sim_norm(b + 2)
                if b:
                    ln_apply(1 + b, pair_of(b - 1))
                if b == 3:
                    x_low(0, 0)
            ln_apply(5, pair_of(3))
            x_low(0, 1)

            def choose(values, taken, width, top, taker, out):
                for n in range(NT):
                    step(ve.max(top8[:, n], values[:, n, 0:width]))
                settled()
                step(ve.tensor_copy(taker[:, :, 0:top], top8[:, :, 0:top]))
                settled()
                for n in range(NT):
                    step(ve.match_replace(taken[:, n], taker[:, n], values[:, n], TAKEN))
                settled()
                step(ve.tensor_tensor(out, taken[:, :, 0:width], values[:, :, 0:width], ALU.not_equal))
                settled()

            def weigh(stage):
                step(ve.tensor_tensor(cw[:, :, 0:E], score[:], chosen[:], ALU.mult))
                settled()
                step(ve.tensor_reduce(wsum[:], cw[:, :, 0:E], AX.X, ALU.add))
                settled()
                if stage:
                    step(ve.tensor_scalar_add(wsum[:], wsum[:], 1e-20))
                    settled()
                step(ve.reciprocal(wsum[:], wsum[:]))
                settled()
                if stage:
                    step(ve.tensor_scalar(wsum[:], wsum[:], ROUTE_SCALE, None, ALU.mult))
                    settled()
                ins = ve.tensor_tensor(cw[:, :, 0:E], cw[:, :, 0:E], over(wsum[:].unsqueeze(2), [P, NT, E]), ALU.mult)
                if stage:
                    ins.then_inc(cw_ready, 1)
                else:
                    step(ins)
                    settled()

            def route_softmax():
                ve.wait_ge(logits_ready, 2)
                step(ve.tensor_copy(logit[:, :, 0:E], bank[2][:, 0:NT * E].rearrange("p (n e) -> p n e", e=E)))
                settled()
                step(ve.tensor_reduce(wsum[:], logit[:, :, 0:E], AX.X, ALU.max))
                settled()
                ve.tensor_tensor(score[:], logit[:, :, 0:E], over(wsum[:].unsqueeze(2), [P, NT, E]),
                                 ALU.subtract).then_inc(lmax_ready, 1)
                choose(logit, mark, E, TOP0, take, chosen[:])
                ve.wait_ge(lexp_ready, 1)
                weigh(0)
                small = cw[:, :, E:E + CHUNKS0]
                step(ve.tensor_tensor(small, cw[:, :, 0:E:2], cw[:, :, 1:E:2], ALU.add))
                settled()
                ve.tensor_scalar(small, small, SMALL_SCALE, None, ALU.mult).then_inc(cw_ready, 1)

            def route_sigmoid(part):
                in_group = pair[:, 0].rearrange("p (n g) -> p n g", g=GROUPS)
                if part == 0:
                    ve.wait_ge(logits_ready, 4)
                    ve.tensor_tensor(score[:], bank[2][:, 0:NT * E].rearrange("p (n e) -> p n e", e=E),
                                     over(router_bias.unsqueeze(1), [P, NT, E]), ALU.add).then_inc(lmax_ready, 1)
                    return
                if part == 1:
                    ve.wait_ge(lexp_ready, 2)
                    step(ve.tensor_scalar_add(score[:], score[:], 1.0))
                    settled()
                    step(ve.reciprocal(score[:], score[:]))
                    settled()
                    s4 = score[:].rearrange("p n (g e) -> p (n g) e", e=E // GROUPS)
                    high0, low0, high1, low1, both, same = (pair[:, i] for i in range(6))
                    step(ve.tensor_tensor(high0, s4[:, :, 0], s4[:, :, 1], ALU.max))
                    step(ve.tensor_tensor(low0, s4[:, :, 0], s4[:, :, 1], ALU.min))
                    step(ve.tensor_tensor(high1, s4[:, :, 2], s4[:, :, 3], ALU.max))
                    step(ve.tensor_tensor(low1, s4[:, :, 2], s4[:, :, 3], ALU.min))
                    settled()
                    step(ve.tensor_tensor(both, high0, high1, ALU.add))
                    step(ve.tensor_tensor(same, high0, low0, ALU.add))
                    step(ve.tensor_tensor(low1, high1, low1, ALU.add))
                    settled()
                    step(ve.tensor_tensor(same, same, low1, ALU.max))
                    settled()
                    step(ve.tensor_tensor(gsum[:, :, 0:GROUPS], both.rearrange("p (n g) -> p n g", g=GROUPS),
                                          same.rearrange("p (n g) -> p n g", g=GROUPS), ALU.max))
                    settled()
                    choose(gsum, gmark, GROUPS, GTOP, gtake, in_group)
                    step(ve.tensor_tensor(logit[:, :, 0:E].rearrange("p n (g e) -> p n g e", g=GROUPS),
                                          score[:].rearrange("p n (g e) -> p n g e", g=GROUPS),
                                          over(in_group.unsqueeze(3), [P, NT, GROUPS, E // GROUPS]), ALU.mult))
                    settled()
                    return
                choose(logit, mark, E, TOP1, take, chosen[:])
                weigh(1)

            def experts(stage):
                def block_act(c, slot, h, first=False, weights="loaded"):
                    blk = 2 * c + h
                    gated, act = product[:, 0], product[:, h if stage else 1]
                    w = cwB[:, slot, h * HALF:(h + 1) * HALF]
                    if weights == "loaded":
                        if stage == 0:
                            ve.wait_ge(cw_in[0][slot], 32 * (c + slot))
                        else:
                            ve.wait_ge(cw_in[1][slot], 8 * (c + (slot - 2)))
                    elif weights == "selected":
                        ve.wait_ge(cwu_ready, 2 * stage + h + 1)
                        w = bank[CWU[stage][h]]
                    if stage == 0:
                        other, last = bank[2 * h + 1], nonlin[:, h]
                        if weights == "selected":
                            other, last = last, other
                            ve.wait_ge(nonlin_done[0], blk + 1)
                        ve.wait_ge(up_ready[0], blk + 1)
                        ve.tensor_tensor(gated, other, w, ALU.mult).then_inc(gated_done[0], 1)
                        ve.wait_ge(gated_done[0], blk + 1)
                        ve.wait_ge(nonlin_done[0], blk + 1)
                        ve.tensor_tensor(act, gated, last, ALU.mult).then_inc(act_done[0], 1)
                    else:
                        ve.wait_ge(nonlin_done[1], blk + 1)
                        if weights == "one":
                            ve.tensor_copy(act, nonlin[:, h]).then_inc(act_done[1], 1)
                        else:
                            ve.tensor_tensor(act, nonlin[:, h], w, ALU.mult).then_inc(act_done[1], 1)
                    ve.wait_ge(act_done[stage], blk + 1)
                    if not first:
                        ve.wait_ge(down_done[stage], blk - 1)
                    ve.tensor_copy(act_hi[:, h], act).then_inc(acthi_done[stage], 1)
                    ve.wait_ge(acthi_done[stage], blk + 1)
                    ve.tensor_tensor(act_lo[:, h], act, act_hi[:, h].bitcast(F32),
                                     ALU.subtract).then_inc(actlo_done[stage], 1)

                if stage == 0:
                    block_act(0, 0, 0, first=True, weights="selected")
                    block_act(0, 0, 1, first=True, weights="selected")
                    block_act(1, 1, 0)
                    block_act(1, 1, 1)
                else:
                    block_act(0, 0, 0, first=True, weights="one")
                    x_low(1, 1)
                    route_sigmoid(0)
                    block_act(0, 0, 1, first=True, weights="one")
                    route_sigmoid(1)
                    block_act(1, 1, 0, weights="one")
                    route_sigmoid(2)
                    block_act(1, 1, 1, weights="one")
                    for h in range(2):
                        block_act(2, 0, h, weights="selected")
                    for h in range(2):
                        block_act(3, 1, h)
                with ve.Fori(2 if stage else 1, NCH[stage] // 2) as i:
                    for slot in range(2):
                        for h in range(2):
                            block_act(2 * i + slot, slot, h)

            def add_y(stage, q):
                ve.wait_ge(down_done[stage], 2 * NCH[stage] - 1 + q // 2)
                xq = x[:, 2 * q:2 * q + 2].rearrange("p n d -> p (n d)")
                ve.scalar_tensor_tensor(xq, bank[4 + q], tanh_g[:, 2 + stage:3 + stage], xq,
                                        ALU.mult, ALU.add).then_inc(x_done[1 + stage], 1)

            route_softmax()
            experts(0)

            def q_split(n):
                q8 = xn[:, n].rearrange("p (j g d) -> p j g d", g=G, d=HD)
                buf = q_tok[:, n % 2]
                ve.wait_ge(xn_ready, 2 * NT + n + 1)
                if n >= 2:
                    ve.wait_ge(qT_ready, 2 * (n - 1))
                ve.tensor_copy(buf[:, :, :, 0:8].bitcast(F32R), q8).then_inc(qtok_ready, 1)
                ve.wait_ge(qtok_ready, 3 * n + 1)
                ve.tensor_tensor(buf[:, :, :, 8:16], q8, buf[:, :, :, 0:8], ALU.subtract).then_inc(qtok_ready, 1)
                ve.tensor_copy(buf[:, :, :, 16:24], buf[:, :, :, 0:8]).then_inc(qtok_ready, 1)

            def unit_max(gs):
                b, jp, st, g = gs // 32, gs // 8 % 4, gs // 4 % 2, gs % 4
                ve.wait_ge(s_ready, gs + 1)
                ve.tensor_reduce(row_max[:, 2 * b + st, 2 * jp:2 * jp + 2, g],
                                 bank[gs % 3].rearrange("p (j t) -> p j t", j=2), AX.X, ALU.max).then_inc(max_done, 1)

            def save_max(mq):
                ve.wait_ge(mT_ready, mq + 1)
                if mq >= 2:
                    ve.wait_ge(mrow_in, 64 * (mq - 1))
                ve.tensor_scalar(neg_mT[:, mq % 2], bank[3][0:QH, 0:S], -1.0, None, ALU.mult).then_inc(mT_saved, 1)

            def add_o(qi):
                b, q = qi // 4, qi % 4
                ve.wait_ge(ot_ready, qi + 1)
                ot = bank[3][:, 0:2 * QH * QW].rearrange("p (s i c) -> p s i c", s=2, c=QW)
                step(ve.reciprocal(o_rec[:], ot[:, :, :, HD]))
                settled()
                ve.tensor_tensor(o_tok[:], ot[:, :, :, 0:HD], over(o_rec[:].unsqueeze(3), [P, 2, QH, HD]),
                                 ALU.mult).then_inc(ot_read, 1)
                ve.wait_ge(ot_read, qi + 1)
                xs = x[:, 2 * b:2 * b + 2, q * QH * HD:(q + 1) * QH * HD]
                ve.scalar_tensor_tensor(xs, o_tok[:].rearrange("p s i d -> p s (i d)"), tanh_g[:, 1:2], xs,
                                        ALU.mult, ALU.add).then_inc(o_added, 1)

            add_y(0, 0)
            ve.wait_ge(x_done[1], 1)
            ln_stats(pair_of(0))
            add_y(0, 1)
            add_y(0, 2)
            add_y(0, 3)
            step(ve.memset(q_tok[:, :, :, :, 24:25], 0.0))
            ln_apply(6, pair_of(0))
            q_split(0)
            q_split(1)
            for gs in range(8):
                unit_max(gs)
            save_max(0)
            ve.wait_ge(x_done[1], 2)
            ln_stats(pair_of(1))
            for gs in range(8, 16):
                unit_max(gs)
            for st in range(NSTEP):
                b, k = st // STEPS, st % STEPS
                ahead = 8 * (st // 4 + 2) + 2 * (st % 4)
                if ahead < 32 * NB:
                    unit_max(ahead)
                    unit_max(ahead + 1)
                ve.wait_ge(exhi_done, st + 1)
                if st >= 3:
                    ve.wait_ge(av_step, st - 2)
                ve.tensor_tensor(ex_lo[:, st % 3, 0], ex[:, st % 2, 0], ex_hi[:, st % 3, 0].bitcast(F32),
                                 ALU.subtract).then_inc(exlo_done, 1)
                if st == 0:
                    ln_apply(7, pair_of(1))
                    q_split(2)
                if st % 4 == 1 and st // 4 + 1 < 4 * NB:
                    save_max(st // 4 + 1)
                if st % 4 == 2 and st > 4:
                    add_o(st // 4 - 1)
                if k == K_STATS and b + 2 < NB:
                    ve.wait_ge(x_done[1], 4)
                    ln_stats(pair_of(b + 2))
                if k == K_APPLY and b + 2 < NB:
                    ln_apply(8 + b, pair_of(b + 2))
                if k == K_SPLIT0 and b + 2 < NB:
                    q_split(2 * b + 4)
                if k == K_SPLIT1 and b + 1 < NB:
                    q_split(2 * b + 3)
                if b == NB - 1:
                    if k == D_STATS:
                        ve.wait_ge(o_added, 8)
                        ln_stats(range(4))
                    if k == D_APPLY:
                        ln_apply(10, range(4))
                    if k == D_FLIP:
                        x_low(1, 0)
                    if k == D_STATS2:
                        ve.wait_ge(o_added, 12)
                        ln_stats((4, 5))
                    if k == D_APPLY2:
                        ln_apply(11, (4, 5))
            add_o(4 * NB - 1)

            ve.wait_ge(o_added, 4 * NB)
            ln_stats((6, 7))
            ln_apply(12, (6, 7))
            experts(1)
            for q in range(4):
                add_y(1, q)


def _layouts(v):
    f = np.float32

    def split_rows(w):
        return w.reshape(KC, P, -1).transpose(1, 0, 2)

    def inner_first(w):
        return w.transpose(1, 0, 2).reshape(D, -1)

    def chunks(up, n):
        return up.reshape(KC, P, n, P).transpose(2, 1, 0, 3).reshape(n, P, KC * P)

    gate = np.concatenate([inner_first(v["L0_ffn_Wg"]), inner_first(v["L0_ffn_cWg"])], 1)
    up = np.concatenate([inner_first(v["L0_ffn_Wu"]), inner_first(v["L0_ffn_cWu"])], 1)
    down = np.concatenate([v["L0_ffn_Wd"].reshape(-1, D), v["L0_ffn_cWd"].reshape(-1, D)], 0)
    w0 = np.concatenate([down.reshape(NC0, P, D), chunks(gate, NC0), chunks(up, NC0)], 2)

    up1 = np.concatenate([v["L1_ffn_Ws1"], v["L1_ffn_W1"].reshape(-1, D)], 0).T
    down1 = np.concatenate([v["L1_ffn_Ws2"].T, v["L1_ffn_W2"].transpose(0, 2, 1).reshape(-1, D)], 0)
    w1 = np.concatenate([down1.reshape(NC1, P, D), chunks(up1, NC1)], 2)

    ctx = v["ctx_512"].reshape(T, CD)
    row = np.concatenate([v["L0_xattn_ln_gamma"], v["L0_xattn_ln_beta"], v["L1_ffn_br"], v["g_xattn"], v["g_ffn"]])
    router = np.stack([split_rows(v["L0_ffn_gate_w"].T), split_rows(v["L1_ffn_Wr"].T)], 1)
    select = np.zeros((GW, 2, P), f)
    select[np.arange(P) // INTER0, 0, np.arange(P)] = 1.0
    select[0, 1] = 1.0
    return {
        "x": v["x"],
        "ctx": v["ctx_512"],
        "ctxT": np.concatenate([ctx.T, np.ones((1, T), f)], 0),
        "wkT": np.concatenate([v["L0_xattn_W_k"].T, v["L0_xattn_b_k"][None]], 0),
        "rows": np.broadcast_to(row, (P, row.size)),
        "router": router,
        "ident": np.eye(P, dtype=f),
        "select": select,
        "w0": w0,
        "w1": w1,
    }


def kernel(**inputs):
    import concourse.bacc as bacc
    from concourse.bass_utils import run_bass_kernel_spmd

    laid = _layouts({k: np.asarray(a) for k, a in inputs.items()})
    nc = bacc.Bacc("TRN2", target_bir_lowering=False, num_devices=1)
    arrays, args = {}, []
    for name, a in laid.items():
        a = np.ascontiguousarray(a)
        arrays[f"in_{name}"] = a
        args.append(nc.dram_tensor(f"in_{name}", a.shape, mybir.dt.from_np(a.dtype), kind="ExternalInput").ap())
    args.append(nc.dram_tensor("out_x", (NB, S, D), F32, kind="ExternalOutput").ap())
    args.append(nc.dram_tensor("cw0_scratch", (NSEG, T), F32).ap())
    args.append(nc.dram_tensor("cw1_scratch", (E, T), F32).ap())
    build(nc, *args)
    r = run_bass_kernel_spmd(nc, [arrays], core_ids=[0])
    return r.results[0]["out_x"]
```

```python
from contextlib import ExitStack

import numpy as np

import concourse.bass as bass
from concourse import mybir

ALU = mybir.AluOpType
ACT = mybir.ActivationFunctionType
AX = mybir.AxisListType
F32 = mybir.dt.float32
F32R = mybir.dt.float32r

P = 128
NB = 4
S = 256
T = NB * S
NT = T // P
HALF = 512
D = 256
KC = D // P
CD = 64
HD = 8
KV = CD // HD
G = D // HD // KV
E = 32
TOP0, TOP1, GROUPS, GTOP = 4, 6, 8, 4
INTER0, CHUNKS0 = 96, 16
SMALL_SCALE = 0.05
ROUTE_SCALE = 2.5
NC0 = E * INTER0 // P + CHUNKS0
NC1 = D // P + E
W0 = 3 * D
W1 = 2 * D
SHARED = D // P
SEG = 32
NSEG = NC0 * P // SEG
GW = E + CHUNKS0
SENT = 3.0e38
TAKEN = -3.0e38
LN_EPS = 1e-5
SIM_EPS = 1e-6
SIM_SCALE = 1.0 / 16.0
QW = 9
QH = 8
WIN = QW * (QH - 1)
SCORE_SCALE = HD ** -0.5


def build(nc, x_d, ctx_d, ctxT_d, wkT_d, rows_d, router_d, ident_d, select_d, w0_d, w1_d, out_d, cw0_d, cw1_d):
    with ExitStack() as ctx:
        def sb(name, shape, dt=F32):
            return ctx.enter_context(nc.sbuf_tensor(name, shape, dt))

        def sem(name):
            return ctx.enter_context(nc.semaphore(name))

        psum = ctx.enter_context(nc.psum_tensor("psum", [P, 8, 512], F32))
        bank = [psum[:, i, :] for i in range(8)]

        with ExitStack() as scope:
            def early(name, shape, dt=F32):
                return scope.enter_context(nc.sbuf_tensor(name, shape, dt))

            ctxT = early("ctxT", [CD + 1, T])
            ctx_tok = early("ctx_tok", [P, NT, KV, HD])
            kv = early("kv", [P, NT, CD])
            kvT = early("kvT", [CD, T])
            xnT = early("xnT", [P, NB, KC, S])
            outT = early("outT", [CD, NB, S])
        qS = sb("qS", [P, KV, T], F32R)
        with ExitStack() as scope:
            vw_hi = scope.enter_context(nc.sbuf_tensor("vw_hi", [P, 2, 2, KV, 2 * WIN + QW], F32R))
            vw_lo = scope.enter_context(nc.sbuf_tensor("vw_lo", [P, 2, 2, KV, 2 * WIN + QW], F32R))
        w_hi = sb("w_hi", [P, 2, W0], F32R)
        w_lo = sb("w_lo", [P, 2, W0], F32R)
        cwB = sb("cwB", [P, 2, T])
        nonlin = sb("nonlin", [P, 2, HALF])
        product = sb("product", [P, 2, HALF])
        act_hi = sb("act_hi", [P, 2, HALF], F32R)
        act_lo = sb("act_lo", [P, 2, HALF], F32R)
        w_raw = sb("w_raw", [P, 2, W0])

        ident = sb("ident", [P, P])
        select = sb("select", [GW, 2, P])
        wkT = sb("wkT", [CD + 1, CD])
        ctx_hi = sb("ctx_hi", [P, NT, KV, HD], F32R)
        ctx_lo = sb("ctx_lo", [P, NT, KV, HD], F32R)
        rows = sb("rows", [P, 2 * D + E + 4])
        gamma, beta = rows[:, 0:D], rows[:, D:2 * D]
        router_bias = rows[:, 2 * D:2 * D + E]
        router = sb("router", [P, 2, KC, E])
        router_hi = sb("router_hi", [P, 2, KC, E], F32R)
        router_lo = sb("router_lo", [P, 2, KC, E], F32R)
        tanh_g = sb("tanh_g", [P, 4])
        half_pow = sb("half_pow", [P, NT])

        x = sb("x", [P, NT, D])
        xn = sb("xn", [P, NT, D])
        xT_hi = sb("xT_hi", [P, KC, T], F32R)
        xT_lo = sb("xT_lo", [P, KC, T], F32R)
        bn = sb("bn", [P, NT, 6])
        mv = sb("mv", [P, NT, 2])
        var = sb("var", [P, NT])
        rstd = sb("rstd", [P, NT])
        neg_max = sb("neg_max", [P, NT])
        exp_sum = sb("exp_sum", [P, NT])
        coef = sb("coef", [P, NT])
        neg_mr = sb("neg_mr", [P, NT])

        logit = sb("logit", [P, NT, E + 4])
        mark = sb("mark", [P, NT, E + 4])
        top8 = sb("top8", [P, NT, 8])
        take = sb("take", [P, NT, 8])
        score = sb("score", [P, NT, E])
        chosen = sb("chosen", [P, NT, E])
        pair = sb("pair", [P, 6, NT * GROUPS])
        gsum = sb("gsum", [P, NT, GROUPS + 4])
        gmark = sb("gmark", [P, NT, GROUPS + 4])
        gtake = sb("gtake", [P, NT, 8])
        wsum = sb("wsum", [P, NT])
        cw = sb("cw", [P, NT, GW])
        cwT = sb("cwT", [GW, T])

        k_tok = sb("k_tok", [P, 2, KV, G, 32])
        q_tok = k_tok
        kS = sb("kS", [P, KV, T], F32R)
        row_max = sb("row_max", [P, NT, KV, G])
        neg_mT = sb("neg_mT", [QH, 2, S], F32R)
        ex = sb("ex", [P, 2, 4, S])
        with ExitStack() as scope:
            k_late = scope.enter_context(nc.sbuf_tensor("k_late", [P, NT // 2, KV, G, 32], F32))
        ex_hi = sb("ex_hi", [P, 3, 4, S], F32R)
        ex_lo = sb("ex_lo", [P, 3, 4, S], F32R)

        def keys(n):
            return k_tok[:, n % 2] if n < NT // 2 else k_late[:, n - NT // 2]

        def kbank(n, jh):
            return bank[(5 if n < NT // 2 else 6) + jh]

        oq = sb("oq", [QW * QH, 2, S])
        o_rec = sb("o_rec", [P, 2, QH])
        o_tok = sb("o_tok", [P, 2, QH, HD])

        ctx_in, ctxtok_in, ident_in, rows_in = sem("ctx_in"), sem("ctxtok_in"), sem("ident_in"), sem("rows_in")
        select_in = sem("select_in")
        x_in = [sem("x_in0"), sem("x_in1")]
        w_in = [[sem("w0_in0"), sem("w0_in1")], [sem("w1_in0"), sem("w1_in1")]]
        mrow_in = sem("mrow_in")
        out_done = sem("out_done")
        chain = sem("chain")
        pool_chain = sem("pool_chain")
        ctx_split = sem("ctx_split")
        router_split = sem("router_split")
        consts_set = sem("consts_set")
        vw_set = sem("vw_set")
        tanh_done = sem("tanh_done")
        kv_ready, kv_saved = sem("kv_ready"), sem("kv_saved")
        ktok_ready, kT_ready, kT_saved = sem("ktok_ready"), sem("kT_ready"), sem("kT_saved")
        var_ready, rstd_ready, xn_ready = sem("var_ready"), sem("rstd_ready"), sem("xn_ready")
        xnT_ready, xnT_saved = sem("xnT_ready"), sem("xnT_saved")
        outT_ready, outT_saved = sem("outT_ready"), sem("outT_saved")
        sim_ready, simvar_ready, simr_ready = sem("sim_ready"), sem("simvar_ready"), sem("simr_ready")
        z_ready, e_ready = sem("z_ready"), sem("e_ready")
        xT_ready, xhi_ready, xlo_ready = sem("xT_ready"), sem("xhi_ready"), sem("xlo_ready")
        logits_ready, lmax_ready, lexp_ready = sem("logits_ready"), sem("lmax_ready"), sem("lexp_ready")
        cw_ready, cwT_ready, cwT_saved = sem("cw_ready"), sem("cwT_ready"), sem("cwT_saved")
        cw_written = [sem("cw_written0"), sem("cw_written1")]
        cw_in = [[sem("cw0_in0"), sem("cw0_in1")], [sem("cw1_in0"), sem("cw1_in1")]]
        lgT_ready, lgT_saved = sem("lgT_ready"), sem("lgT_saved")
        mr_ready = sem("mr_ready")
        late_set = sem("late_set")
        relu_done, square_done = sem("relu_done"), sem("square_done")
        cwu_ready, cwu_saved = sem("cwu_ready"), sem("cwu_saved")
        exp_loaded = sem("exp_loaded")

        def two(name):
            return [sem(name + "0"), sem(name + "1")]

        whi_done, wlo_done = two("whi_done"), two("wlo_done")
        gate_ready, up_ready = two("gate_ready"), two("up_ready")
        nonlin_done, gated_done, act_done = two("nonlin_done"), two("gated_done"), two("act_done")
        acthi_done, actlo_done, down_done = two("acthi_done"), two("actlo_done"), two("down_done")
        qtok_ready, qT_ready, qT_saved = sem("qtok_ready"), sem("qT_ready"), sem("qT_saved")
        s_ready, max_done = sem("s_ready"), sem("max_done")
        mT_ready, mT_saved = sem("mT_ready"), sem("mT_saved")
        exhi_done, exlo_done, exlo2_done = sem("exhi_done"), sem("exlo_done"), sem("exlo2_done")
        st_ready, exp_done, av_step = sem("st_ready"), sem("exp_done"), sem("av_step")
        oq_saved, ot_ready, ot_read, o_added = sem("oq_saved"), sem("ot_ready"), sem("ot_read"), sem("o_added")
        x_done = [sem("x_done_A"), sem("x_done_B"), sem("x_done_D")]

        NCH = [NC0, NC1]
        WCOL = [W0, W1]
        XBANK = [[0, 1, 4, 2], [0, 1, 6, 7]]
        LTBANK = [(3, 7), (0, 1)]
        CWB = [(5, 7), (3, 2)]
        CWU = [(4, 6), (3, 2)]
        DONE0 = [0, 2 * SHARED]
        STEPS = 16
        NSTEP = NB * STEPS
        STATS_AT, APPLY_AT = {0: 1}, {1: 1}
        SPLIT_AT = {1: 2, 3: 3}
        QFLIP_AT = {2: 4, 3: 5, 5: 6, 7: 7}
        for nb in range(2, NB):
            at = (nb - 2) * STEPS
            STATS_AT[at + 6], APPLY_AT[at + 8] = nb, nb
            SPLIT_AT[at + 13], SPLIT_AT[at + 17] = 2 * nb, 2 * nb + 1
            for k in range(4):
                QFLIP_AT[at + (15, 17, 19, 21)[k]] = 4 * nb + k

        def ex_dve(step):
            return 2 if step == NSTEP - 1 else 1

        K_FLIP_AT = (2, 5, 8, 11)
        QBANK = (4, 3, 4, 3)
        D_STATS, D_APPLY, D_FLIP, D_LOGITS, D_STATS2, D_APPLY2, D_ROUTE = 4, 6, 8, 9, 9, 11, 10

        block = ctx.enter_context(nc.Block())

        @block.sync
        def _(sp):
            sp.dma_start(ctxT[:], ctxT_d).then_inc(ctx_in, 16)
            sp.dma_start(wkT[:], wkT_d).then_inc(ctx_in, 16)
            xt = x_d.rearrange("b (s p) d -> p (b s) d", p=P)
            sp.dma_start(x[:, 4:8], xt[:, 4:8]).then_inc(x_in[1], 16)
            sp.dma_start(rows[:], rows_d).then_inc(rows_in, 16)
            sp.dma_start(router[:], router_d).then_inc(rows_in, 16)
            sp.dma_start(select[:], select_d).then_inc(select_in, 16)

            def load(stage, c, slot):
                src = (w0_d, w1_d)[stage]
                sp.dma_start(w_raw[:, slot, 0:WCOL[stage]], src[c]).then_inc(w_in[stage][slot], 16)

            def load_cw(stage, c, slot):
                if stage == 0:
                    for s in range(P // SEG):
                        row = cw0_d[bass.ds(c * (P // SEG) + s, 1), :]
                        sp.dma_start(cwB[s * SEG:(s + 1) * SEG, slot, :],
                                     row.broadcast_to([SEG, T])).then_inc(cw_in[0][slot], 16)
                else:
                    row = cw1_d[bass.ds(c - SHARED, 1), :]
                    sp.dma_start(cwB[:, slot, :], row.broadcast_to([P, T])).then_inc(cw_in[1][slot], 16)

            def first_loads(stage):
                for slot in range(2):
                    if stage:
                        sp.wait_ge(wlo_done[0], NC0 - 1 + 2 * slot)
                    load(stage, slot, slot)

            def other_loads(stage, first):
                with sp.Fori(first, NCH[stage] // 2) as i:
                    for slot in range(2):
                        sp.wait_ge(wlo_done[stage], 2 * i + (slot - 1))
                        load(stage, 2 * i + slot, slot)
                        sp.wait_ge(gated_done[stage], 4 * i + (2 * slot - 2) - DONE0[stage])
                        load_cw(stage, 2 * i + slot, slot)

            first_loads(0)
            sp.wait_ge(cw_written[0], 64)
            load_cw(0, 1, 1)
            other_loads(0, 1)
            first_loads(1)
            for mq in range(4 * NB):
                b, q = mq // 4, mq % 4
                sp.wait_ge(mT_saved, mq + 1)
                for jj in range(2):
                    sp.dma_start(qS[24:P:32, 2 * q + jj, b * S:(b + 1) * S].bitcast(F32),
                                 neg_mT[G * jj:G * (jj + 1), mq % 2, :].bitcast(F32)).then_inc(mrow_in, 16)
            for c in (2, 3):
                sp.wait_ge(wlo_done[1], c - 1)
                load(1, c, c % 2)
            sp.wait_ge(cw_written[1], 32)
            load_cw(1, 3, 1)
            other_loads(1, 2)
            ot = out_d.rearrange("b (s p) d -> p (b s) d", p=P)
            for q in range(4):
                sp.wait_ge(x_done[2], q + 1)
                sp.dma_start(ot[:, 2 * q:2 * q + 2], x[:, 2 * q:2 * q + 2]).then_inc(out_done, 16)
            sp.wait_ge(out_done, 64)

        @block.gpsimd
        def _(pool):
            pool.memset(half_pow[:], -0.5).then_inc(pool_chain, 1)
            pool.wait_ge(pool_chain, 1)

            def ln_rstd(group, tiles):
                pool.wait_ge(var_ready, group + 1)
                a, b = tiles[0], tiles[-1] + 1
                pool.tensor_tensor(rstd[:, a:b], var[:, a:b], half_pow[:, 0:b - a], ALU.pow).then_inc(rstd_ready, 1)

            def w_low(stage, c, slot, a=0, b=None):
                b = b or WCOL[stage]
                pool.wait_ge(whi_done[stage], c + 1)
                pool.tensor_tensor(w_lo[:, slot, a:b], w_raw[:, slot, a:b],
                                   w_hi[:, slot, a:b].bitcast(F32), ALU.subtract).then_inc(wlo_done[stage], 1)

            for h in range(2):
                ln_rstd(h, range(4 * h, 4 * h + 4))

            def sim_rstd(b):
                pool.wait_ge(simvar_ready, b + 1)
                pool.tensor_tensor(rstd[:, 2 * b:2 * b + 2], var[:, 2 * b:2 * b + 2],
                                   half_pow[:, 0:2], ALU.pow).then_inc(simr_ready, 1)

            for b in range(NB):
                sim_rstd(b)
            w_low(0, 0, 0)
            for b in range(NB):
                ln_rstd(2 + b, (2 * b, 2 * b + 1))
                if b < NB - 1:
                    n2 = slice(2 * b, 2 * b + 2)
                    pool.wait_ge(rstd_ready, 3 + b)
                    pool.tensor_tensor(neg_mr[:, n2], neg_mr[:, n2], rstd[:, n2], ALU.mult).then_inc(mr_ready, 1)
            w_low(0, 1, 1)
            with pool.Fori(1, NC0 // 2 - 1) as i:
                for slot in range(2):
                    w_low(0, 2 * i + slot, slot)
            w_low(0, NC0 - 2, 0)
            w_low(0, NC0 - 1, 1, D, W0)
            w_low(0, NC0, 1, 0, D)

            ln_rstd(6, (0, 1))
            pool.wait_ge(down_done[0], 2 * NC0)
            pool.memset(vw_hi[:].bitcast(F32), 0.0).then_inc(pool_chain, 1)
            pool.memset(vw_lo[:].bitcast(F32), 0.0).then_inc(pool_chain, 1)
            pool.wait_ge(pool_chain, 3)
            pool.memset(vw_hi[:, :, :, :, WIN + HD:WIN + QW].bitcast(F32), 1.0).then_inc(vw_set, 1)

            def values(b):
                if b >= 2:
                    pool.wait_ge(av_step, STEPS * (b - 1))
                for tc in range(2):
                    for vw, part in ((vw_hi, ctx_hi), (vw_lo, ctx_lo)):
                        pool.tensor_copy(vw[:, b % 2, tc, :, WIN:WIN + HD],
                                         part[:, 2 * b + tc].bitcast(F32)).then_inc(vw_set, 1)

            values(0)
            ln_rstd(7, (2, 3))
            for step in range(NSTEP):
                b, k = step // STEPS, step % STEPS
                pool.wait_ge(exhi_done, step + 1)
                if step >= 3:
                    pool.wait_ge(av_step, step - 2)
                pool.tensor_tensor(ex_lo[:, step % 3, ex_dve(step):], ex[:, step % 2, ex_dve(step):],
                                   ex_hi[:, step % 3, ex_dve(step):].bitcast(F32), ALU.subtract).then_inc(exlo2_done, 1)
                if step in STATS_AT and step:
                    ln_rstd(6 + STATS_AT[step], (2 * STATS_AT[step], 2 * STATS_AT[step] + 1))
                if b == NB - 1 and k in (D_STATS, D_STATS + 1):
                    ln_rstd(10 + k - D_STATS, (2 * (k - D_STATS), 2 * (k - D_STATS) + 1))
                if b == NB - 1 and k == D_STATS2:
                    ln_rstd(12, (4, 5))
                if k == 4 and b + 1 < NB:
                    values(b + 1)

            def shared_low(blk):
                pool.wait_ge(acthi_done[1], blk + 1)
                if blk >= 2:
                    pool.wait_ge(down_done[1], blk - 1)
                pool.tensor_tensor(act_lo[:, blk % 2], nonlin[:, blk % 2], act_hi[:, blk % 2].bitcast(F32),
                                   ALU.subtract).then_inc(actlo_done[1], 1)

            w_low(1, 0, 0)
            ln_rstd(13, (6, 7))
            shared_low(0)
            w_low(1, 1, 1)
            shared_low(1)
            shared_low(2)
            w_low(1, 2, 0)
            shared_low(3)
            w_low(1, 3, 1)
            with pool.Fori(2, NC1 // 2) as i:
                for slot in range(2):
                    w_low(1, 2 * i + slot, slot)

        @block.scalar
        def _(sc):
            xt = x_d.rearrange("b (s p) d -> p (b s) d", p=P)
            sc.dma_start(x[:, 0:4], xt[:, 0:4]).then_inc(x_in[0], 16)
            sc.dma_start(ctx_tok[:], ctx_d.rearrange("b (s p) (j d) -> p (b s) j d", p=P, d=HD)).then_inc(ctxtok_in, 16)
            sc.dma_start(ident[:], ident_d).then_inc(ident_in, 16)

            def k_split(n):
                if n == 0:
                    sc.wait_ge(ctx_split, 2)
                    sc.wait_ge(consts_set, 2)
                if n >= NT // 2:
                    sc.wait_ge(late_set, 2)
                elif n >= 2:
                    sc.wait_ge(kT_ready, 2 * (n - 1))
                for part, src in ((0, ctx_hi), (1, ctx_hi), (2, ctx_lo)):
                    sc.activation(keys(n)[:, :, :, 8 * part:8 * part + 8],
                                  src[:, n].bitcast(F32).unsqueeze(2).broadcast_to([P, KV, G, HD]),
                                  ACT.Copy).then_inc(ktok_ready, 1)

            def k_save(n):
                for jh in range(2):
                    sc.wait_ge(kT_ready, 2 * n + jh + 1)
                    sc.activation(kS[:, 4 * jh:4 * jh + 4, n * P:(n + 1) * P],
                                  kbank(n, jh).rearrange("p (j t) -> p j t", j=4), ACT.Copy).then_inc(kT_saved, 1)

            sc.wait_ge(rows_in, 32)
            sc.activation(tanh_g[:], rows[:, 2 * D + E:2 * D + E + 4], ACT.Tanh).then_inc(tanh_done, 1)

            def kv_save(h):
                sc.wait_ge(kv_ready, 2 * h + 1)
                sc.activation(kvT[:, h * HALF:(h + 1) * HALF], bank[h][0:CD, :], ACT.Copy).then_inc(kv_saved, 1)
                sc.wait_ge(kv_ready, 2 * h + 2)
                sc.activation(kv[:, 4 * h:4 * h + 4].rearrange("p n c -> p (n c)"), bank[(2, 5)[h]][:, 0:4 * CD],
                              ACT.Copy).then_inc(kv_saved, 1)

            def xnT_save(b):
                sc.wait_ge(xnT_ready, b + 1)
                sc.activation(xnT[:, b].rearrange("p k s -> p (k s)"), bank[3 + b % 2],
                              ACT.Copy).then_inc(xnT_saved, 1)

            kv_save(0)
            xnT_save(0)
            for b in range(NB):
                if b == 1:
                    kv_save(1)
                sc.wait_ge(outT_ready, b + 1)
                sc.activation(outT[:, b], bank[7][0:CD, 0:S], ACT.Copy).then_inc(outT_saved, 1)
                if b + 1 < NB:
                    xnT_save(b + 1)

            def w_high(stage, c, slot, a=0, b=None):
                b = b or WCOL[stage]
                sc.wait_ge(w_in[stage][slot], 8 * (c - slot) + 16)
                sc.activation(w_hi[:, slot, a:b], w_raw[:, slot, a:b], ACT.Copy).then_inc(whi_done[stage], 1)

            def x_high(stage, h):
                for k in range(KC):
                    u = 2 * h + k
                    sc.wait_ge(xT_ready, 4 * stage + u + 1)
                    sc.activation(xT_hi[:, k, h * HALF:(h + 1) * HALF], bank[XBANK[stage][u]],
                                  ACT.Copy).then_inc(xhi_ready, 1)

            def save_logits(stage, h):
                sc.wait_ge(lgT_ready, 2 * stage + h + 1)
                sc.activation(cwT[0:E, h * HALF:(h + 1) * HALF], bank[LTBANK[stage][h]][0:E, :],
                              ACT.Copy).then_inc(lgT_saved, 1)

            def silu(c, h, first=False):
                blk = 2 * c + h
                sc.wait_ge(gate_ready[0], blk + 1)
                if not first:
                    sc.wait_ge(act_done[0], blk - 1)
                sc.activation(nonlin[:, h], bank[2 * h], ACT.Silu).then_inc(nonlin_done[0], 1)

            def next_high(stage, c, slot, first=False):
                if not first:
                    sc.wait_ge(down_done[stage], 2 * c)
                w_high(stage, c + 1, 1 - slot)

            def experts(stage):
                def one(c, slot, last=False):
                    if stage == 0:
                        silu(c, 0)
                    if not last:
                        next_high(stage, c, slot)
                    if stage == 0:
                        silu(c, 1)

                if stage == 0:
                    one(1, 1)
                    k_split(NT // 2)
                with sc.Fori(1, NCH[stage] // 2 - 1) as i:
                    one(2 * i, 0)
                    one(2 * i + 1, 1)
                last = NCH[stage] - 1
                if stage:
                    one(last - 1, 0)
                    one(last, 1, last=True)
                    return
                sc.wait_ge(up_ready[0], 2 * last - 2)
                w_high(0, last, 1, D, W0)
                silu(last - 1, 0)
                sc.wait_ge(down_done[0], 2 * last - 2)
                w_high(0, last, 1, 0, D)
                silu(last - 1, 1)
                k_split(NT // 2 + 1)
                silu(last, 0)
                k_split(NT // 2 + 2)
                silu(last, 1)
                k_split(NT // 2 + 3)

            def save_cw(stage, h):
                half = slice(h * HALF, (h + 1) * HALF)
                n = 2 * stage + h + 1
                sc.wait_ge(cwT_ready, n)
                sc.activation(cwT[:, half], bank[CWB[stage][h]][0:GW, :], ACT.Copy).then_inc(cwT_saved, 1)
                sc.wait_ge(cwT_saved, n)
                if stage:
                    sc.dma_start(cw1_d[:, half], cwT[0:E, half]).then_inc(cw_written[1], 16)
                    return
                big = INTER0 // SEG
                small = P // SEG
                sc.dma_start(cw0_d[0:E * big, half].rearrange("(e r) t -> e r t", r=big),
                             cwT[0:E, half].unsqueeze(1).broadcast_to([E, big, HALF])).then_inc(cw_written[0], 16)
                sc.dma_start(cw0_d[E * big:NSEG, half].rearrange("(e r) t -> e r t", r=small),
                             cwT[E:GW, half].unsqueeze(1).broadcast_to([CHUNKS0, small, HALF]))\
                    .then_inc(cw_written[0], 16)

            def save_spread(stage, h):
                sc.wait_ge(cwu_ready, 2 * stage + h + 1)
                sc.activation(cwB[:, 0, h * HALF:(h + 1) * HALF], bank[CWU[stage][h]], ACT.Copy).then_inc(cwu_saved, 1)

            def route_exp(group):
                sc.wait_ge(lmax_ready, group + 1)
                part = score[:] if group == 0 else score[:, 4 * group - 4:4 * group]
                sc.activation(part, part, ACT.Exp, scale=-1.0 if group else 1.0).then_inc(lexp_ready, 1)

            def exponentials(b):
                sc.wait_ge(z_ready, b + 1)
                for n in (2 * b, 2 * b + 1):
                    sc.activation(xn[:, n], xn[:, n], ACT.Exp, bias=neg_max[:, n:n + 1],
                                  accum_out=exp_sum[:, n:n + 1]).then_inc(e_ready, 1)

            def norm(b):
                sc.wait_ge(mr_ready, b + 1)
                for n in (2 * b, 2 * b + 1):
                    sc.activation(xn[:, n], x[:, n], ACT.Identity, bias=neg_mr[:, n:n + 1],
                                  scale=rstd[:, n:n + 1]).then_inc(xn_ready, 1)

            k_split(0)
            exponentials(0)
            k_save(0)
            k_split(1)
            exponentials(1)
            k_save(1)
            w_high(0, 0, 0)
            k_split(2)
            norm(0)
            k_save(2)
            k_split(3)
            exponentials(2)
            k_save(3)
            norm(1)
            exponentials(3)
            norm(2)

            for h in range(2):
                x_high(0, h)
            for h in range(2):
                save_logits(0, h)
            route_exp(0)
            silu(0, 0, first=True)
            next_high(0, 0, 0, first=True)
            silu(0, 1, first=True)
            for h in range(2):
                save_cw(0, h)
            for h in range(2):
                save_spread(0, h)
            experts(0)

            def q_save(u):
                n, jh = u // 2, u % 2
                sc.wait_ge(qT_ready, u + 1)
                src = bank[QBANK[u] if u < 4 else 3]
                sc.activation(qS[:, 4 * jh:4 * jh + 4, n * P:(n + 1) * P],
                              src.rearrange("p (j t) -> p j t", j=4), ACT.Copy).then_inc(qT_saved, 1)

            def save_oq(qi):
                sc.wait_ge(av_step, 4 * (qi + 1))
                if qi >= 2:
                    sc.wait_ge(ot_ready, qi - 1)
                sc.activation(oq[:, qi % 2], bank[6 + qi % 2][0:QW * QH, 0:S], ACT.Copy).then_inc(oq_saved, 1)

            sc.activation(coef[:, 0:1], half_pow[:, 0:1], ACT.Exp).then_inc(exp_loaded, 1)

            def shared(blk):
                h = blk % 2
                sc.wait_ge(gate_ready[1], blk + 1)
                if blk >= 2:
                    sc.wait_ge(actlo_done[1], blk - 1)
                sc.activation(nonlin[:, h], bank[h], ACT.Relu).then_inc(relu_done, 1)
                sc.wait_ge(relu_done, blk + 1)
                sc.activation(nonlin[:, h], nonlin[:, h], ACT.Square).then_inc(square_done, 1)
                sc.wait_ge(square_done, blk + 1)
                if blk >= 2:
                    sc.wait_ge(down_done[1], blk - 1)
                sc.activation(act_hi[:, h], nonlin[:, h], ACT.Copy).then_inc(acthi_done[1], 1)

            for u in range(4):
                q_save(u)
            for n in range(NT // 2, NT):
                k_save(n)
            for step in range(NSTEP):
                b, k = step // STEPS, step % STEPS
                sc.wait_ge(st_ready, step + 1)
                if step >= 2:
                    sc.wait_ge(exlo_done, step - 1)
                    sc.wait_ge(exlo2_done, step - 1)
                sc.activation(ex[:, step % 2], psum[:, 4:6, :].rearrange("p g (j s) -> p (g j) s", j=2), ACT.Exp,
                              scale=SCORE_SCALE).then_inc(exp_done, 1)
                sc.wait_ge(exp_done, step + 1)
                if step >= 3:
                    sc.wait_ge(av_step, step - 2)
                sc.activation(ex_hi[:, step % 3], ex[:, step % 2], ACT.Copy).then_inc(exhi_done, 1)
                if step in QFLIP_AT:
                    q_save(QFLIP_AT[step])
                if step % 4 == 1 and step > 4:
                    save_oq(step // 4 - 1)
                if b == NB - 1 and k == D_FLIP:
                    x_high(1, 0)
                if b == NB - 1 and k == D_LOGITS:
                    save_logits(1, 0)
                if b == NB - 1 and k == D_ROUTE + 1:
                    route_exp(1)
            save_oq(4 * NB - 1)

            sc.wait_ge(av_step, NSTEP)
            w_high(1, 0, 0)
            shared(0)
            x_high(1, 1)
            save_logits(1, 1)
            next_high(1, 0, 0, first=True)
            route_exp(2)
            shared(1)
            save_cw(1, 0)
            shared(2)
            save_spread(1, 0)
            next_high(1, 1, 1)
            shared(3)
            save_cw(1, 1)
            save_spread(1, 1)
            experts(1)

        @block.tensor
        def _(pe):
            def flip(out, src, inc=None):
                n = src.shape[0]
                ins = pe.transpose(out, src, ident[0:n, 0:n])
                if inc is not None:
                    ins.then_inc(inc, 1)

            def kv_mm(h):
                pe.matmul(bank[h][0:CD, :], wkT[:], ctxT[:, h * HALF:(h + 1) * HALF],
                          start=True, stop=True).then_inc(kv_ready, 1)
                for n in range(4 * h, 4 * h + 4):
                    last = pe.matmul(bank[(2, 5)[h]][:, n % 4 * CD:(n % 4 + 1) * CD], ctxT[:, n * P:(n + 1) * P],
                                     wkT[:], start=True, stop=True)
                last.then_inc(kv_ready, 1)

            pe.wait_ge(ctx_in, 32)
            kv_mm(0)
            pe.wait_ge(ident_in, 16)

            def k_flip(n):
                pe.wait_ge(ktok_ready, 3 * (n + 1))
                for jh in range(2):
                    if n:
                        pe.wait_ge(kT_saved, 2 * n + jh - 1)
                    for jj in range(4):
                        src = keys(n)[:, 4 * jh + jj].rearrange("p g c -> p (g c)")
                        flip(kbank(n, jh)[:, jj * P:(jj + 1) * P], src, kT_ready if jj == 3 else None)

            def xn_flip(b):
                pe.wait_ge(xn_ready, 2 * b + 2)
                if b >= 2:
                    pe.wait_ge(xnT_saved, b - 1)
                for k in range(KC):
                    for st in range(2):
                        u = 2 * k + st
                        flip(bank[3 + b % 2][:, u * P:(u + 1) * P], xn[:, 2 * b + st, k * P:(k + 1) * P],
                             xnT_ready if u == 3 else None)

            def out_mm(b):
                pe.wait_ge(xnT_saved, b + 1)
                pe.wait_ge(kv_saved, 2 if b < 2 else 4)
                if b:
                    pe.wait_ge(outT_saved, b)
                for k in range(KC):
                    last = pe.matmul(bank[7][0:CD, 0:S], kv[:, 2 * b + k], xnT[:, b, k],
                                     start=(k == 0), stop=(k == KC - 1))
                last.then_inc(outT_ready, 1)

            def sim_mm(b):
                pe.wait_ge(outT_saved, b + 1)
                if b == 1:
                    pe.wait_ge(kv_saved, 4)
                for st in range(2):
                    last = pe.matmul(bank[b][:, st * S:(st + 1) * S], outT[:, b, st * P:(st + 1) * P],
                                     kvT[:, b * S:(b + 1) * S], start=True, stop=True)
                last.then_inc(sim_ready, 1)

            xn_flip(0)
            for b in range(NB):
                out_mm(b)
                if b + 1 < NB:
                    xn_flip(b + 1)
                sim_mm(b)
                if b == 0:
                    kv_mm(1)
            for n in range(NT // 2):
                k_flip(n)

            def x_flip(stage, h):
                if stage and h == 0:
                    pe.wait_ge(max_done, 32 * NB)
                for k in range(KC):
                    u = 2 * h + k
                    pe.wait_ge(xn_ready, (2 * stage + 1) * NT + 4 * h + 4)
                    for tt in range(4):
                        flip(bank[XBANK[stage][u]][:, tt * P:(tt + 1) * P], xn[:, 4 * h + tt, k * P:(k + 1) * P],
                             xT_ready if tt == 3 else None)

            def logits(stage, h):
                pe.wait_ge(router_split, 2)
                pe.wait_ge(xlo_ready, 4 * stage + 2 * h + 2)
                m = 0
                for rp, xp in ((router_hi, xT_hi), (router_lo, xT_hi), (router_hi, xT_lo)):
                    for k in range(KC):
                        last = pe.matmul(bank[LTBANK[stage][h]][0:E, :], rp[:, stage, k, :],
                                         xp[:, k, h * HALF:(h + 1) * HALF], start=(m == 0), stop=(m == 5))
                        m += 1
                last.then_inc(lgT_ready, 1)

            def logits_flip(stage, h):
                pe.wait_ge(lgT_saved, 2 * stage + h + 1)
                if stage:
                    pe.wait_ge(lmax_ready, 1 + h)
                for n in range(4 * h, 4 * h + 4):
                    flip(bank[2][:, n * E:(n + 1) * E], cwT[0:E, n * P:(n + 1) * P],
                         logits_ready if n % 4 == 3 else None)

            def experts(stage):
                def inner(out, col, slot, h, done):
                    m = 0
                    for wp, xp in ((w_hi, xT_hi), (w_hi, xT_lo), (w_lo, xT_hi)):
                        for k in range(KC):
                            last = pe.matmul(out, wp[:, slot, col + k * P:col + (k + 1) * P],
                                             xp[:, k, h * HALF:(h + 1) * HALF], start=(m == 0), stop=(m == 5))
                            m += 1
                    last.then_inc(done[stage], 1)

                def flip_cw(hh):
                    pe.wait_ge(cw_ready, (1, 2 + hh)[stage])
                    for tt in range(4):
                        flip(bank[CWB[stage][hh]][0:GW, tt * P:(tt + 1) * P], cw[:, 4 * hh + tt],
                             cwT_ready if tt == 3 else None)

                def spread_cw(hh):
                    if hh == 0:
                        pe.wait_ge(select_in, 16)
                    pe.wait_ge(cwT_saved, 2 * stage + hh + 1)
                    pe.matmul(bank[CWU[stage][hh]], select[:, stage, :], cwT[:, hh * HALF:(hh + 1) * HALF],
                              start=True, stop=True).then_inc(cwu_ready, 1)

                def down(blk, slot, h, first=False, final=False, p=None):
                    p = h if p is None else p
                    pe.wait_ge(acthi_done[stage], blk + 1)
                    for m, (ap, wp) in enumerate(((act_hi, w_hi), (act_hi, w_lo), (act_lo, w_hi))):
                        if m == 2:
                            pe.wait_ge(actlo_done[stage], blk + 1)
                        for tt in range(4):
                            n = 4 * h + tt
                            last = pe.matmul(bank[4 + n // 2][:, (n % 2) * D:(n % 2 + 1) * D],
                                             ap[:, p, tt * P:(tt + 1) * P], wp[:, slot, 0:D],
                                             start=first and n % 2 == 0 and m == 0, stop=final and m == 2,
                                             skip_group_check=True)
                    last.then_inc(down_done[stage], 1)

                def block_in(c, slot, h, first, shared_before=False):
                    blk = 2 * c + h
                    if h == 0:
                        pe.wait_ge(whi_done[stage], c + 1)
                        pe.wait_ge(wlo_done[stage], c + 1)
                    banks_free(blk, first, shared_before)
                    products_in(slot, h, h)

                def banks_free(blk, first=False, shared_before=False):
                    if first:
                        return
                    if stage == 0:
                        pe.wait_ge(nonlin_done[0], blk - 1)
                        pe.wait_ge(gated_done[0], blk - 1)
                    elif shared_before:
                        pe.wait_ge(relu_done, blk - 1)
                    else:
                        pe.wait_ge(act_done[1], blk - 1 - DONE0[1])

                def products_in(slot, h, p):
                    if stage:
                        inner(bank[p], D, slot, h, gate_ready)
                    else:
                        inner(bank[2 * p], D, slot, h, gate_ready)
                        inner(bank[2 * p + 1], 2 * D, slot, h, up_ready)

                def chunk(c, slot):
                    for h in range(2):
                        block_in(c, slot, h, False)
                        down(2 * c + h - 1, slot if h else 1 - slot, 1 - h)

                if stage == 0:
                    block_in(0, 0, 0, True)
                    pe.wait_ge(lmax_ready, 1)
                    block_in(0, 0, 1, True)
                    pe.wait_ge(kT_saved, NT)
                    for hh in range(2):
                        flip_cw(hh)
                    for hh in range(2):
                        spread_cw(hh)
                    down(0, 0, 0, first=True)
                    block_in(1, 1, 0, False)
                    down(1, 0, 1, first=True)
                    block_in(1, 1, 1, False)
                    down(2, 1, 0)
                else:
                    block_in(0, 0, 0, True)
                    x_flip(1, 1)
                    logits(1, 1)
                    down(0, 0, 0, first=True)
                    logits_flip(1, 1)
                    block_in(0, 0, 1, True)
                    flip_cw(0)
                    block_in(1, 1, 0, False, shared_before=True)
                    spread_cw(0)
                    down(1, 0, 1, first=True)
                    block_in(1, 1, 1, False, shared_before=True)
                    down(2, 1, 0)
                    pe.wait_ge(lmax_ready, 3)
                    flip_cw(1)
                    block_in(2, 0, 0, False, shared_before=True)
                    spread_cw(1)
                    down(3, 1, 1)
                    block_in(2, 0, 1, False, shared_before=True)
                    down(4, 0, 0)
                    chunk(3, 1)
                with pe.Fori(2 if stage else 1, NCH[stage] // 2 - (1 - stage)) as i:
                    chunk(2 * i, 0)
                    chunk(2 * i + 1, 1)
                if stage:
                    down(2 * NCH[1] - 1, 1, 1, final=True)
                    return
                last = NC0 - 1
                for n, (slot, h) in enumerate(((0, 0), (1, 0), (0, 1), (1, 1))):
                    blk = 2 * last - 2 + n
                    if n < 2:
                        pe.wait_ge(whi_done[0], last + n)
                        pe.wait_ge(wlo_done[0], last + n)
                    banks_free(blk)
                    products_in(slot, h, n % 2)
                    if n == 2:
                        pe.wait_ge(whi_done[0], NC0 + 1)
                        pe.wait_ge(wlo_done[0], NC0 + 1)
                    before = ((1, 1, 1, False), (0, 0, 0, False), (1, 0, 1, True), (0, 1, 0, False))[n]
                    down(blk - 1, before[0], before[1], p=before[2], final=before[3])
                down(2 * NC0 - 1, 1, 1, final=True)

            for h in range(2):
                x_flip(0, h)
            for h in range(2):
                logits(0, h)
            for h in range(2):
                logits_flip(0, h)
            experts(0)

            flips = {"q": 0, "m": 0, "o": 0}

            def bank3_free():
                pe.wait_ge(qT_saved, flips["q"])
                if flips["m"]:
                    pe.wait_ge(mT_saved, flips["m"])
                if flips["o"]:
                    pe.wait_ge(ot_read, flips["o"])

            def q_flip(u):
                n, jh = u // 2, u % 2
                pe.wait_ge(qtok_ready, 3 * (n + 1))
                if u >= 4:
                    bank3_free()
                elif u >= 2:
                    pe.wait_ge(qT_saved, u - 1)
                for jj in range(4):
                    src = q_tok[:, n % 2, 4 * jh + jj].rearrange("p g c -> p (g c)")
                    to = bank[QBANK[u] if u < 4 else 3]
                    flip(to[:, jj * P:(jj + 1) * P], src, qT_ready if jj == 3 else None)
                flips["q"] += 1

            def s_mm(gs):
                b, jp, st, g = gs // 32, gs // 8 % 4, gs // 4 % 2, gs % 4
                pe.wait_ge(qT_saved, 2 * (2 * b + st + 1))
                if gs >= 3:
                    pe.wait_ge(max_done, gs - 2)
                for jj in range(2):
                    j = 2 * jp + jj
                    last = pe.matmul(bank[gs % 3][:, jj * S:(jj + 1) * S],
                                     qS[32 * g:32 * g + 32, j, (2 * b + st) * P:(2 * b + st + 1) * P],
                                     kS[32 * g:32 * g + 32, j, b * S:(b + 1) * S], start=True, stop=True)
                last.then_inc(s_ready, 1)

            def max_flip(mq):
                b, q = mq // 4, mq % 4
                pe.wait_ge(max_done, 8 * (mq + 1))
                bank3_free()
                for st in range(2):
                    flip(bank[3][0:QH, st * P:(st + 1) * P],
                         row_max[:, 2 * b + st, 2 * q:2 * q + 2].rearrange("p j g -> p (j g)"),
                         mT_ready if st == 1 else None)
                flips["m"] += 1

            def st_mm(step):
                b, q, gp, tc = step // STEPS, step // 4 % 4, step // 2 % 2, step % 2
                if step % 4 == 0:
                    pe.wait_ge(mrow_in, 32 * (step // 4 + 1))
                if step:
                    pe.wait_ge(exp_done, step)
                for jj in range(2):
                    for gi in range(2):
                        g, j = 2 * gp + gi, 2 * q + jj
                        last = pe.matmul(bank[4 + gi][:, jj * S:(jj + 1) * S],
                                         kS[32 * g:32 * g + 32, j, b * S + tc * P:b * S + (tc + 1) * P],
                                         qS[32 * g:32 * g + 32, j, b * S:(b + 1) * S], start=True, stop=True)
                last.then_inc(st_ready, 1)

            def av_mm(step):
                b, q, gp, tc = step // STEPS, step // 4 % 4, step // 2 % 2, step % 2
                qi = step // 4
                pe.wait_ge(exlo_done, step + 1)
                pe.wait_ge(exlo2_done, step + 1)
                if step == 0:
                    pe.wait_ge(kT_saved, 2 * NT)
                if step % STEPS == 0:
                    pe.wait_ge(vw_set, 4 * b + 5)
                if step % 4 == 0 and qi >= 2:
                    pe.wait_ge(oq_saved, qi - 1)
                m = 0
                for gi in range(2):
                    for jj in range(2):
                        at = WIN - QW * (4 * jj + 2 * gp + gi)
                        for vp, ep in ((vw_hi, ex_hi), (vw_lo, ex_hi), (vw_hi, ex_lo)):
                            last = pe.matmul(bank[6 + qi % 2][0:QW * QH, 0:S],
                                             vp[:, b % 2, tc, 2 * q + jj, at:at + QW * QH],
                                             ep[:, step % 3, 2 * gi + jj, :],
                                             start=(step % 4 == 0 and m == 0), stop=(step % 4 == 3 and m == 11))
                            m += 1
                last.then_inc(av_step, 1)

            def o_flip(qi):
                pe.wait_ge(oq_saved, qi + 1)
                bank3_free()
                for st in range(2):
                    flip(bank[3][:, st * QW * QH:(st + 1) * QW * QH], oq[:, qi % 2, st * P:(st + 1) * P],
                         ot_ready if st == 1 else None)
                flips["o"] += 1

            for u in range(4):
                q_flip(u)
            for gs in range(8):
                s_mm(gs)
                if gs == 1:
                    pe.wait_ge(x_done[1], 4)
                if gs in K_FLIP_AT:
                    k_flip(NT // 2 + K_FLIP_AT.index(gs))
            max_flip(0)
            for gs in range(8, 15):
                s_mm(gs)
                if gs in K_FLIP_AT:
                    k_flip(NT // 2 + K_FLIP_AT.index(gs))
            st_mm(0)
            for gs in range(15, 16):
                s_mm(gs)
            for step in range(NSTEP):
                b, k = step // STEPS, step % STEPS
                if step:
                    st_mm(step)
                ahead = 8 * (step // 4 + 2) + 2 * (step % 4)
                if ahead < 32 * NB:
                    s_mm(ahead)
                    s_mm(ahead + 1)
                if step >= 2:
                    av_mm(step - 2)
                if step in QFLIP_AT:
                    q_flip(QFLIP_AT[step])
                if step % 4 == 0 and step // 4 + 1 < 4 * NB:
                    max_flip(step // 4 + 1)
                if step % 4 == 2 and step > 4:
                    o_flip(step // 4 - 1)
                if b == NB - 1 and k == D_FLIP:
                    x_flip(1, 0)
                if b == NB - 1 and k == D_LOGITS:
                    logits(1, 0)
                if b == NB - 1 and k == D_ROUTE:
                    logits_flip(1, 0)
            av_mm(NSTEP - 2)
            av_mm(NSTEP - 1)
            o_flip(4 * NB - 1)

            experts(1)

        @block.vector
        def _(ve):
            steps = [0]

            def step(ins):
                ins.then_inc(chain, 1)
                steps[0] += 1

            def settled():
                ve.wait_ge(chain, steps[0])

            def over(ap, shape):
                return ap.broadcast_to(shape)

            ve.memset(k_tok[:, :, :, :, 24:32], 0.0).then_inc(consts_set, 1)
            ve.wait_ge(consts_set, 1)
            ve.memset(k_tok[:, :, :, :, 24:25], 1.0).then_inc(consts_set, 1)

            def ln_stats(tiles, negative=False):
                for n in tiles:
                    step(ve.bn_stats(bn[:, n], x[:, n]))
                settled()
                for n in tiles:
                    step(ve.bn_aggr(mv[:, n], bn[:, n]))
                settled()
                a, b = tiles[0], tiles[-1] + 1
                if negative:
                    step(ve.tensor_scalar(neg_mr[:, a:b], mv[:, a:b, 0], -1.0, None, ALU.mult))
                ve.tensor_scalar_add(var[:, a:b], mv[:, a:b, 1], LN_EPS).then_inc(var_ready, 1)

            def ln_apply(group, tiles):
                ve.wait_ge(rstd_ready, group + 1)
                for n in tiles:
                    ve.tensor_scalar(xn[:, n], x[:, n], mv[:, n, 0:1], rstd[:, n:n + 1],
                                     ALU.subtract, ALU.mult).then_inc(xn_ready, 1)

            def pair_of(b):
                return (2 * b, 2 * b + 1)

            for h in range(2):
                ve.wait_ge(x_in[h], 16)
                ln_stats(range(4 * h, 4 * h + 4))
                ln_apply(h, range(4 * h, 4 * h + 4))

            def sim_stats(b):
                ve.wait_ge(sim_ready, b + 1)
                for st in range(2):
                    step(ve.bn_stats(bn[:, 2 * b + st], bank[b][:, st * S:(st + 1) * S]))
                settled()
                for st in range(2):
                    step(ve.bn_aggr(mv[:, 2 * b + st], bn[:, 2 * b + st]))
                settled()
                ve.tensor_scalar_add(var[:, 2 * b:2 * b + 2], mv[:, 2 * b:2 * b + 2, 1],
                                     SIM_EPS / SIM_SCALE ** 2).then_inc(simvar_ready, 1)

            def sim_norm(b):
                ve.wait_ge(simr_ready, b + 1)
                for st in range(2):
                    n = 2 * b + st
                    step(ve.scalar_tensor_tensor(xn[:, n], bank[b][:, st * S:(st + 1) * S], mv[:, n, 0:1], gamma,
                                                 ALU.subtract, ALU.mult))
                settled()
                for st in range(2):
                    n = 2 * b + st
                    step(ve.scalar_tensor_tensor(xn[:, n], xn[:, n], rstd[:, n:n + 1], beta, ALU.mult, ALU.add))
                settled()
                ve.tensor_reduce(neg_max[:, 2 * b:2 * b + 2], xn[:, 2 * b:2 * b + 2], AX.X, ALU.max,
                                 negate=True).then_inc(z_ready, 1)

            def sim_add(b):
                ve.wait_ge(e_ready, 2 * b + 2)
                ve.wait_ge(tanh_done, 1)
                step(ve.reciprocal(coef[:, 2 * b:2 * b + 2], exp_sum[:, 2 * b:2 * b + 2]))
                settled()
                step(ve.tensor_scalar(coef[:, 2 * b:2 * b + 2], coef[:, 2 * b:2 * b + 2], tanh_g[:, 0:1], None,
                                      ALU.mult))
                settled()
                for n in (2 * b, 2 * b + 1):
                    ve.scalar_tensor_tensor(x[:, n], xn[:, n], coef[:, n:n + 1], x[:, n],
                                            ALU.mult, ALU.add).then_inc(x_done[0], 1)

            def x_low(stage, h):
                for k in range(KC):
                    u = 2 * h + k
                    ve.wait_ge(xhi_ready, 4 * stage + u + 1)
                    ve.tensor_tensor(xT_lo[:, k, h * HALF:(h + 1) * HALF], bank[XBANK[stage][u]],
                                     xT_hi[:, k, h * HALF:(h + 1) * HALF].bitcast(F32),
                                     ALU.subtract).then_inc(xlo_ready, 1)

            sim_stats(0)
            ve.wait_ge(ctxtok_in, 16)
            ve.tensor_copy(ctx_hi[:], ctx_tok[:]).then_inc(ctx_split, 1)
            ve.wait_ge(ctx_split, 1)
            ve.tensor_tensor(ctx_lo[:], ctx_tok[:], ctx_hi[:].bitcast(F32), ALU.subtract).then_inc(ctx_split, 1)
            step(ve.memset(logit[:, :, E:], SENT))
            step(ve.memset(gsum[:, :, GROUPS:], SENT))
            step(ve.memset(take[:], SENT))
            step(ve.memset(gtake[:], SENT))
            step(ve.memset(cw[:], 0.0))
            ve.wait_ge(rows_in, 32)
            ve.tensor_copy(router_hi[:], router[:]).then_inc(router_split, 1)
            ve.wait_ge(router_split, 1)
            ve.tensor_tensor(router_lo[:], router[:], router_hi[:].bitcast(F32), ALU.subtract).then_inc(router_split, 1)
            sim_stats(1)
            sim_norm(0)
            sim_stats(2)
            sim_norm(1)
            sim_stats(3)
            for b in range(NB):
                sim_add(b)
                ve.wait_ge(x_done[0], 2 * b + 2)
                ln_stats(pair_of(b), negative=b < NB - 1)
                if b + 2 < NB:
                    sim_norm(b + 2)
            x_low(0, 0)
            ln_apply(5, pair_of(3))
            x_low(0, 1)

            def choose(values, taken, width, top, taker, out, a, b):
                for n in range(a, b):
                    step(ve.max(top8[:, n], values[:, n, 0:width]))
                settled()
                step(ve.tensor_copy(taker[:, a:b, 0:top], top8[:, a:b, 0:top]))
                settled()
                for n in range(a, b):
                    step(ve.match_replace(taken[:, n], taker[:, n], values[:, n], TAKEN))
                settled()
                step(ve.tensor_tensor(out[:, a:b], taken[:, a:b, 0:width], values[:, a:b, 0:width], ALU.not_equal))
                settled()

            def weigh(stage, a, b):
                part, total = cw[:, a:b, 0:E], wsum[:, a:b]
                step(ve.tensor_tensor(part, score[:, a:b], chosen[:, a:b], ALU.mult))
                settled()
                step(ve.tensor_reduce(total, part, AX.X, ALU.add))
                settled()
                if stage:
                    step(ve.tensor_scalar_add(total, total, 1e-20))
                    settled()
                step(ve.reciprocal(total, total))
                settled()
                if stage:
                    step(ve.tensor_scalar(total, total, ROUTE_SCALE, None, ALU.mult))
                    settled()
                ins = ve.tensor_tensor(part, part, over(total.unsqueeze(2), [P, b - a, E]), ALU.mult)
                if stage:
                    ins.then_inc(cw_ready, 1)
                else:
                    step(ins)
                    settled()

            def route_softmax():
                ve.wait_ge(logits_ready, 2)
                step(ve.tensor_copy(logit[:, :, 0:E], bank[2][:, 0:NT * E].rearrange("p (n e) -> p n e", e=E)))
                settled()
                step(ve.tensor_reduce(wsum[:], logit[:, :, 0:E], AX.X, ALU.max))
                settled()
                ve.tensor_tensor(score[:], logit[:, :, 0:E], over(wsum[:].unsqueeze(2), [P, NT, E]),
                                 ALU.subtract).then_inc(lmax_ready, 1)
                choose(logit, mark, E, TOP0, take, chosen, 0, NT)
                ve.wait_ge(lexp_ready, 1)
                weigh(0, 0, NT)
                small = cw[:, :, E:E + CHUNKS0]
                step(ve.tensor_tensor(small, cw[:, :, 0:E:2], cw[:, :, 1:E:2], ALU.add))
                settled()
                ve.tensor_scalar(small, small, SMALL_SCALE, None, ALU.mult).then_inc(cw_ready, 1)

            def route_sigmoid(h, part):
                a, b = 4 * h, 4 * h + 4
                s, n4 = score[:, a:b], 4 * GROUPS
                in_group = pair[:, 0].rearrange("p (n g) -> p n g", g=GROUPS)
                if part == 0:
                    ve.wait_ge(logits_ready, 3 + h)
                    ve.tensor_tensor(s, bank[2][:, a * E:b * E].rearrange("p (n e) -> p n e", e=E),
                                     over(router_bias.unsqueeze(1), [P, b - a, E]), ALU.add).then_inc(lmax_ready, 1)
                if part == 1:
                    ve.wait_ge(lexp_ready, 2 + h)
                    step(ve.tensor_scalar_add(s, s, 1.0))
                    settled()
                    step(ve.reciprocal(s, s))
                    settled()
                    s4 = s.rearrange("p n (g e) -> p (n g) e", e=E // GROUPS)
                    high0, low0, high1, low1, both, same = (pair[:, i, 0:n4] for i in range(6))
                    step(ve.tensor_tensor(high0, s4[:, :, 0], s4[:, :, 1], ALU.max))
                    step(ve.tensor_tensor(low0, s4[:, :, 0], s4[:, :, 1], ALU.min))
                    step(ve.tensor_tensor(high1, s4[:, :, 2], s4[:, :, 3], ALU.max))
                    step(ve.tensor_tensor(low1, s4[:, :, 2], s4[:, :, 3], ALU.min))
                    settled()
                    step(ve.tensor_tensor(both, high0, high1, ALU.add))
                    step(ve.tensor_tensor(same, high0, low0, ALU.add))
                    step(ve.tensor_tensor(low1, high1, low1, ALU.add))
                    settled()
                    step(ve.tensor_tensor(same, same, low1, ALU.max))
                    settled()
                    step(ve.tensor_tensor(gsum[:, a:b, 0:GROUPS], both.rearrange("p (n g) -> p n g", g=GROUPS),
                                          same.rearrange("p (n g) -> p n g", g=GROUPS), ALU.max))
                    settled()
                if part == 2:
                    choose(gsum, gmark, GROUPS, GTOP, gtake, in_group, a, b)
                    step(ve.tensor_tensor(logit[:, a:b, 0:E].rearrange("p n (g e) -> p n g e", g=GROUPS),
                                          s.rearrange("p n (g e) -> p n g e", g=GROUPS),
                                          over(in_group[:, a:b].unsqueeze(3), [P, b - a, GROUPS, E // GROUPS]),
                                          ALU.mult))
                    settled()
                if part == 3:
                    choose(logit, mark, E, TOP1, take, chosen, a, b)
                if part == 4:
                    weigh(1, a, b)

            def add_y(stage, q):
                n = 2 * NCH[stage]
                ve.wait_ge(down_done[stage], n if q // 2 else (n - 2, n - 1)[stage])
                xq = x[:, 2 * q:2 * q + 2].rearrange("p n d -> p (n d)")
                ve.scalar_tensor_tensor(xq, bank[4 + q], tanh_g[:, 2 + stage:3 + stage], xq,
                                        ALU.mult, ALU.add).then_inc(x_done[1 + stage], 1)

            def experts(stage):
                def block_act(c, slot, h, first=False, weights="loaded", blk=None, p=None):
                    if blk is None:
                        blk, p = 2 * c + h, h
                    gated, act = product[:, 0], product[:, 1]
                    w = cwB[:, slot, h * HALF:(h + 1) * HALF]
                    if weights == "loaded":
                        if stage == 0:
                            ve.wait_ge(cw_in[0][slot], 32 * (c + slot))
                        else:
                            ve.wait_ge(cw_in[1][slot], 8 * (c + (slot - 2)))
                    elif weights == "selected":
                        ve.wait_ge(cwu_saved, 2 * stage + h + 1)
                    if stage == 0:
                        ve.wait_ge(up_ready[0], blk + 1)
                        ve.tensor_tensor(gated, bank[2 * p + 1], w, ALU.mult).then_inc(gated_done[0], 1)
                        ve.wait_ge(gated_done[0], blk + 1)
                        ve.wait_ge(nonlin_done[0], blk + 1)
                        ve.tensor_tensor(act, gated, nonlin[:, p], ALU.mult).then_inc(act_done[0], 1)
                    else:
                        ve.wait_ge(gate_ready[1], blk + 1)
                        ve.scalar_tensor_tensor(gated, bank[p], 0.0, w, ALU.max, ALU.mult).then_inc(gated_done[1], 1)
                        ve.wait_ge(gated_done[1], blk + 1 - DONE0[1])
                        ve.scalar_tensor_tensor(act, bank[p], 0.0, gated, ALU.max, ALU.mult).then_inc(act_done[1], 1)
                    if not first:
                        ve.wait_ge(down_done[stage], blk - 1)
                    ve.wait_ge(act_done[stage], blk + 1 - DONE0[stage])
                    ve.tensor_copy(act_hi[:, p], act).then_inc(acthi_done[stage], 1)
                    ve.wait_ge(acthi_done[stage], blk + 1)
                    ve.tensor_tensor(act_lo[:, p], act, act_hi[:, p].bitcast(F32),
                                     ALU.subtract).then_inc(actlo_done[stage], 1)

                if stage == 0:
                    block_act(0, 0, 0, first=True, weights="selected")
                    block_act(0, 0, 1, first=True, weights="selected")
                    block_act(1, 1, 0)
                    block_act(1, 1, 1)
                    ve.memset(k_late[:, :, :, :, 24:32], 0.0).then_inc(late_set, 1)
                    ve.wait_ge(late_set, 1)
                    ve.memset(k_late[:, :, :, :, 24:25], 1.0).then_inc(late_set, 1)
                else:
                    x_low(1, 1)
                    for part in range(5):
                        route_sigmoid(1, part)
                    ve.wait_ge(actlo_done[1], 2 * SHARED)
                    for h in range(2):
                        block_act(2, 0, h, weights="selected")
                    for h in range(2):
                        block_act(3, 1, h)
                with ve.Fori(2 if stage else 1, NCH[stage] // 2 - (1 - stage)) as i:
                    for slot in range(2):
                        for h in range(2):
                            block_act(2 * i + slot, slot, h)
                if stage:
                    return
                for n, (slot, h) in enumerate(((0, 0), (1, 0), (0, 1), (1, 1))):
                    if n == 3:
                        add_y(0, 0)
                        step(ve.memset(q_tok[:, :, :, :, 24:25], 0.0))
                        ve.wait_ge(x_done[1], 1)
                        ln_stats(pair_of(0))
                    block_act(NC0 - 2 + slot, slot, h, blk=2 * NC0 - 4 + n, p=n % 2)

            route_softmax()
            experts(0)

            def q_split(n):
                q8 = xn[:, n].rearrange("p (j g d) -> p j g d", g=G, d=HD)
                buf = q_tok[:, n % 2]
                ve.wait_ge(xn_ready, 2 * NT + n + 1)
                if n >= 2:
                    ve.wait_ge(qT_ready, 2 * (n - 1))
                ve.tensor_copy(buf[:, :, :, 0:8].bitcast(F32R), q8).then_inc(qtok_ready, 1)
                ve.wait_ge(qtok_ready, 3 * n + 1)
                ve.tensor_tensor(buf[:, :, :, 8:16], q8, buf[:, :, :, 0:8], ALU.subtract).then_inc(qtok_ready, 1)
                ve.tensor_copy(buf[:, :, :, 16:24], buf[:, :, :, 0:8]).then_inc(qtok_ready, 1)

            def unit_max(gs):
                b, jp, st, g = gs // 32, gs // 8 % 4, gs // 4 % 2, gs % 4
                ve.wait_ge(s_ready, gs + 1)
                ve.tensor_reduce(row_max[:, 2 * b + st, 2 * jp:2 * jp + 2, g],
                                 bank[gs % 3].rearrange("p (j t) -> p j t", j=2), AX.X, ALU.max).then_inc(max_done, 1)

            def save_max(mq):
                ve.wait_ge(mT_ready, mq + 1)
                if mq >= 2:
                    ve.wait_ge(mrow_in, 32 * (mq - 1))
                ve.tensor_scalar(neg_mT[:, mq % 2], bank[3][0:QH, 0:S], -1.0, None, ALU.mult).then_inc(mT_saved, 1)

            def add_o(qi):
                b, q = qi // 4, qi % 4
                ve.wait_ge(ot_ready, qi + 1)
                ot = bank[3][:, 0:2 * QH * QW].rearrange("p (s i c) -> p s i c", s=2, c=QW)
                step(ve.reciprocal(o_rec[:], ot[:, :, :, HD]))
                settled()
                ve.tensor_tensor(o_tok[:], ot[:, :, :, 0:HD], over(o_rec[:].unsqueeze(3), [P, 2, QH, HD]),
                                 ALU.mult).then_inc(ot_read, 1)
                ve.wait_ge(ot_read, qi + 1)
                xs = x[:, 2 * b:2 * b + 2, q * QH * HD:(q + 1) * QH * HD]
                ve.scalar_tensor_tensor(xs, o_tok[:].rearrange("p s i d -> p s (i d)"), tanh_g[:, 1:2], xs,
                                        ALU.mult, ALU.add).then_inc(o_added, 1)

            ln_apply(6, pair_of(0))
            q_split(0)
            q_split(1)
            for q in range(1, 4):
                add_y(0, q)
            for gs in range(8):
                unit_max(gs)
            save_max(0)
            for gs in range(8, 16):
                unit_max(gs)
            for st in range(NSTEP):
                b, k = st // STEPS, st % STEPS
                ahead = 8 * (st // 4 + 2) + 2 * (st % 4)
                if ahead < 32 * NB:
                    unit_max(ahead)
                    unit_max(ahead + 1)
                ve.wait_ge(exhi_done, st + 1)
                if st >= 3:
                    ve.wait_ge(av_step, st - 2)
                ve.tensor_tensor(ex_lo[:, st % 3, 0:ex_dve(st)], ex[:, st % 2, 0:ex_dve(st)],
                                 ex_hi[:, st % 3, 0:ex_dve(st)].bitcast(F32), ALU.subtract).then_inc(exlo_done, 1)
                if st % 4 == 0 and st // 4 + 1 < 4 * NB:
                    save_max(st // 4 + 1)
                if st % 4 == 2 and st > 4:
                    add_o(st // 4 - 1)
                if st in STATS_AT:
                    ve.wait_ge(x_done[1], 4)
                    ln_stats(pair_of(STATS_AT[st]))
                if st in APPLY_AT:
                    ln_apply(6 + APPLY_AT[st], pair_of(APPLY_AT[st]))
                if st in SPLIT_AT:
                    q_split(SPLIT_AT[st])
                if b == NB - 1:
                    if k in (D_STATS, D_STATS + 1):
                        ve.wait_ge(o_added, 8)
                        ln_stats(pair_of(k - D_STATS))
                    if k in (D_APPLY, D_APPLY + 1):
                        ln_apply(10 + k - D_APPLY, pair_of(k - D_APPLY))
                    if k == D_FLIP:
                        x_low(1, 0)
                    if k == D_STATS2:
                        ve.wait_ge(o_added, 12)
                        ln_stats((4, 5))
                    if k == D_APPLY2:
                        ln_apply(12, (4, 5))
                    if D_ROUTE <= k < D_ROUTE + 4:
                        route_sigmoid(0, k - D_ROUTE)
                    if k == STEPS - 1:
                        route_sigmoid(0, 4)
            add_o(4 * NB - 1)

            ve.wait_ge(o_added, 4 * NB)
            ln_stats((6, 7))
            ln_apply(13, (6, 7))
            experts(1)
            for q in range(4):
                add_y(1, q)


def _layouts(v):
    f = np.float32

    def split_rows(w):
        return w.reshape(KC, P, -1).transpose(1, 0, 2)

    def inner_first(w):
        return w.transpose(1, 0, 2).reshape(D, -1)

    def chunks(up, n):
        return up.reshape(KC, P, n, P).transpose(2, 1, 0, 3).reshape(n, P, KC * P)

    gate = np.concatenate([inner_first(v["L0_ffn_Wg"]), inner_first(v["L0_ffn_cWg"])], 1)
    up = np.concatenate([inner_first(v["L0_ffn_Wu"]), inner_first(v["L0_ffn_cWu"])], 1)
    down = np.concatenate([v["L0_ffn_Wd"].reshape(-1, D), v["L0_ffn_cWd"].reshape(-1, D)], 0)
    w0 = np.concatenate([down.reshape(NC0, P, D), chunks(gate, NC0), chunks(up, NC0)], 2)

    up1 = np.concatenate([v["L1_ffn_Ws1"], v["L1_ffn_W1"].reshape(-1, D)], 0).T
    down1 = np.concatenate([v["L1_ffn_Ws2"].T, v["L1_ffn_W2"].transpose(0, 2, 1).reshape(-1, D)], 0)
    w1 = np.concatenate([down1.reshape(NC1, P, D), chunks(up1, NC1)], 2)

    ctx = v["ctx_512"].reshape(T, CD)
    row = np.concatenate([v["L0_xattn_ln_gamma"], v["L0_xattn_ln_beta"], v["L1_ffn_br"], v["g_xattn"], v["g_ffn"]])
    router = np.stack([split_rows(v["L0_ffn_gate_w"].T), split_rows(v["L1_ffn_Wr"].T)], 1)
    select = np.zeros((GW, 2, P), f)
    select[np.arange(P) // INTER0, 0, np.arange(P)] = 1.0
    select[0, 1] = 1.0
    return {
        "x": v["x"],
        "ctx": v["ctx_512"],
        "ctxT": np.concatenate([ctx.T, np.ones((1, T), f)], 0),
        "wkT": np.concatenate([v["L0_xattn_W_k"].T, v["L0_xattn_b_k"][None]], 0),
        "rows": np.broadcast_to(row, (P, row.size)),
        "router": router,
        "ident": np.eye(P, dtype=f),
        "select": select,
        "w0": w0,
        "w1": w1,
    }


def kernel(**inputs):
    import concourse.bacc as bacc
    from concourse.bass_utils import run_bass_kernel_spmd

    laid = _layouts({k: np.asarray(a) for k, a in inputs.items()})
    nc = bacc.Bacc("TRN2", target_bir_lowering=False, num_devices=1)
    arrays, args = {}, []
    for name, a in laid.items():
        a = np.ascontiguousarray(a)
        arrays[f"in_{name}"] = a
        args.append(nc.dram_tensor(f"in_{name}", a.shape, mybir.dt.from_np(a.dtype), kind="ExternalInput").ap())
    args.append(nc.dram_tensor("out_x", (NB, S, D), F32, kind="ExternalOutput").ap())
    args.append(nc.dram_tensor("cw0_scratch", (NSEG, T), F32).ap())
    args.append(nc.dram_tensor("cw1_scratch", (E, T), F32).ap())
    build(nc, *args)
    r = run_bass_kernel_spmd(nc, [arrays], core_ids=[0])
    return r.results[0]["out_x"]
```
